# Optimizing a Trainium2 kernel written in Bass

```python
import numpy as np
import jax
import jax.numpy as jnp

def _softmax(x, axis=-1):
    return jax.nn.softmax(x, axis=axis)

def _gelu(x):
    return jax.nn.gelu(x, approximate=True)

def _silu(x):
    return jax.nn.silu(x)

def _sigmoid(x):
    return jax.nn.sigmoid(x)

def _layernorm(x, axis=-1, eps=1e-05):
    m = jnp.mean(x, axis=axis, keepdims=True)
    v = jnp.var(x, axis=axis, keepdims=True)
    return (x - m) / jnp.sqrt(v + eps)

def _scatter_add(tgt, idx, src, axis=0):
    return tgt.at[idx].add(src)

def _segment_sum(src, seg, n):
    return jax.ops.segment_sum(src, seg, n)
kernel_name = 'mk_perceiver_d1_seqx_r2_b80c9c'

def setup_inputs(seed: int=0):
    np.random.seed(seed)
    _w = jnp.asarray

    def _rec_inputs():
        import jax
        import jax.numpy as jnp
        _rk = jax.random.key(seed)
        x = -0.0003929 + 0.9999 * jax.random.normal(jax.random.fold_in(_rk, 1), (4, 128, 512), jnp.float32)
        _lenS = 128 - jax.random.randint(jax.random.fold_in(_rk, 7), (4,), 0, max(1, 128 // 4) + 1, jnp.int32)
        _lenS2 = 2048 - jax.random.randint(jax.random.fold_in(_rk, 8), (4,), 0, max(1, 2048 // 4) + 1, jnp.int32)
        _ctx_512P = jax.random.normal(jax.random.fold_in(_rk, 11), (4, 16, 256), jnp.float32)
        _ctx_512c = jax.random.dirichlet(jax.random.fold_in(_rk, 511), 0.3 * jnp.ones((16,), jnp.float32), (4, 2048))
        _ctx_512t = jnp.einsum('bsk,bkd->bsd', _ctx_512c, _ctx_512P)
        _ctx_512t = _ctx_512t * jax.lax.rsqrt(jnp.mean(jnp.square(_ctx_512t)) + 1e-12) * 0.953939
        ctx_512 = -1.39393e-06 + 0.999914 * (_ctx_512t + 0.3 * jax.random.normal(jax.random.fold_in(_rk, 611), (4, 2048, 256), jnp.float32))
        return (x, ctx_512)
    x, ctx_512 = _rec_inputs()

    def _L0_xattn_setup():
        import jax, jax.numpy as jnp
        import numpy as np
        HEADS = 16
        D_MODEL = 512
        IMG_MODEL = 256
        D_K = D_MODEL // HEADS
        key = jax.random.key(seed)
        ks = jax.random.split(key, 12)
        B, LQ, LKV = (8, 1024, 512)
        s_dm = 1.0 / np.sqrt(D_MODEL)
        s_im = 1.0 / np.sqrt(IMG_MODEL)
        return {'q': jax.random.normal(ks[0], (B, LQ, D_MODEL), jnp.float32), 'k': jax.random.normal(ks[1], (B, LKV, IMG_MODEL), jnp.float32), 'v': jax.random.normal(ks[2], (B, LKV, IMG_MODEL), jnp.float32), 'Wq': jax.random.normal(ks[3], (D_MODEL, D_MODEL), jnp.float32) * s_dm, 'bq': jnp.zeros((D_MODEL,), jnp.float32), 'Wk': jax.random.normal(ks[4], (IMG_MODEL, D_MODEL), jnp.float32) * s_im, 'bk': jnp.zeros((D_MODEL,), jnp.float32), 'Wv': jax.random.normal(ks[5], (IMG_MODEL, D_MODEL), jnp.float32) * s_im, 'bv': jnp.zeros((D_MODEL,), jnp.float32), 'Wo': jax.random.normal(ks[6], (D_MODEL, D_MODEL), jnp.float32) * s_dm, 'bo': jnp.zeros((D_MODEL,), jnp.float32)}
    _L0_xattn_all = _L0_xattn_setup()
    _L0_xattn_in = {k: v for k, v in _L0_xattn_all.items() if k in ('Wq', 'bq', 'Wk', 'bk', 'Wv', 'bv', 'Wo', 'bo')}
    del _L0_xattn_all

    def _L0_attn_setup():
        import jax, jax.numpy as jnp
        import numpy as np
        D_MODEL, N_HEADS, N_KV, HEAD_DIM, D_LAT = (512, 8, 2, 128, 32)
        N_REP = N_HEADS // N_KV
        B, T = (2, 1024)
        key = jax.random.key(seed)
        ks = jax.random.split(key, 8)
        s = lambda fan_in: 1.0 / np.sqrt(fan_in)
        return {'x': jax.random.normal(ks[0], (B, T, D_MODEL), jnp.float32), 'wq': jax.random.normal(ks[1], (D_MODEL, N_HEADS * HEAD_DIM), jnp.float32) * s(D_MODEL), 'wk_down': jax.random.normal(ks[2], (D_MODEL, N_KV * D_LAT), jnp.float32) * s(D_MODEL), 'wv_down': jax.random.normal(ks[3], (D_MODEL, N_KV * D_LAT), jnp.float32) * s(D_MODEL), 'wk_up': jax.random.normal(ks[4], (D_LAT, HEAD_DIM), jnp.float32) * s(D_LAT), 'wv_up': jax.random.normal(ks[5], (D_LAT, HEAD_DIM), jnp.float32) * s(D_LAT), 'wo': jax.random.normal(ks[6], (N_HEADS * HEAD_DIM, D_MODEL), jnp.float32) * s(N_HEADS * HEAD_DIM)}
    _L0_attn_all = _L0_attn_setup()
    _L0_attn_in = {k: v for k, v in _L0_attn_all.items() if k in ('wq', 'wk_down', 'wv_down', 'wk_up', 'wv_up', 'wo')}
    del _L0_attn_all

    def _L0_ffn_setup():
        import jax, jax.numpy as jnp
        import numpy as np
        DIM = 512
        DEPTH = 6
        HEADS = 16
        DIM_HEAD = 64
        WINDOW = 128
        INNER = HEADS * DIM_HEAD
        DIM_INNER = int(DIM * 4 * 2 / 3)
        QK_SCALE = 8.0

        def shift_tokens(t):
            a, s = jnp.split(t, 2, -1)
            s = jnp.pad(s, ((0, 0), (1, 0), (0, 0)))[:, :-1]
            return jnp.concatenate([a, s], -1)

        def l2norm(t):
            return t / jnp.maximum(jnp.linalg.norm(t, axis=-1, keepdims=True), 1e-12)

        def rotate_half(x):
            x1, x2 = jnp.split(x, 2, -1)
            return jnp.concatenate([-x2, x1], -1)

        def rotary_tables(n):
            half = jnp.arange(0, DIM_HEAD, 2, dtype=jnp.float32)
            inv_freq = 1.0 / 10000.0 ** (half / DIM_HEAD)
            t = jnp.arange(n, dtype=jnp.float32)
            freqs = t[:, None] * inv_freq[None, :]
            freqs = jnp.concatenate([freqs, freqs], -1)
            base_scale = (half + 0.4 * DIM_HEAD) / (1.4 * DIM_HEAD)
            power = (t - n // 2) / (WINDOW // 2)
            scale = base_scale[None, :] ** power[:, None]
            scale = jnp.concatenate([scale, scale], -1)
            return (freqs, scale)

        def local_attention(q, k, v):
            b, h, n, d = q.shape
            w = WINDOW
            nw = n // w
            bq = q.reshape(b, h, nw, w, d)
            bk = k.reshape(b, h, nw, w, d)
            bv = v.reshape(b, h, nw, w, d)

            def look(t):
                p = jnp.pad(t, ((0, 0), (0, 0), (1, 0), (0, 0), (0, 0)))
                return jnp.concatenate([p[:, :, :nw], p[:, :, 1:]], axis=3)
            bk2, bv2 = (look(bk), look(bv))
            seq = jnp.arange(n).reshape(nw, w)
            seq_p = jnp.pad(seq, ((1, 0), (0, 0)), constant_values=-1)
            jt = jnp.concatenate([seq_p[:nw], seq_p[1:]], axis=1)
            it = seq[:, :, None]
            jb = jt[:, None, :]
            mask = (it < jb) | (it > jb + w) | (jb == -1)
            sim = jnp.einsum('bhwie,bhwje->bhwij', bq, bk2) * QK_SCALE
            sim = jnp.where(mask, -jnp.finfo(sim.dtype).max, sim)
            attn = jax.nn.softmax(sim, -1)
            out = jnp.einsum('bhwij,bhwje->bhwie', attn, bv2)
            return out.reshape(b, h, n, d)

        def attn_layer(x, Wqkv, qs, ksc, Wo):
            b, n, _ = x.shape
            qkv = x @ Wqkv
            q, k, v = jnp.split(qkv, 3, -1)
            sh = lambda t: t.reshape(b, n, HEADS, DIM_HEAD).transpose(0, 2, 1, 3)
            q, k, v = (sh(q), sh(k), sh(v))
            q = l2norm(q) * qs
            k = l2norm(k) * ksc
            freqs, scale = rotary_tables(n)
            cos, sin = (jnp.cos(freqs), jnp.sin(freqs))
            q = q * cos * scale + rotate_half(q) * sin * scale
            inv = 1.0 / scale
            k = k * cos * inv + rotate_half(k) * sin * inv
            out = local_attention(q, k, v)
            out = out.transpose(0, 2, 1, 3).reshape(b, n, INNER)
            return out @ Wo

        def ffn_layer(x, g, bln, W1, b1, W2, b2):
            mu = x.mean(-1, keepdims=True)
            var = ((x - mu) ** 2).mean(-1, keepdims=True)
            xn = (x - mu) / jnp.sqrt(var + 1e-05) * g + bln
            hg = xn @ W1 + b1
            a, gate = jnp.split(hg, 2, -1)
            return a * jax.nn.gelu(gate, approximate=False) @ W2 + b2
        key = jax.random.key(seed)
        ks = jax.random.split(key, 8)
        B, N = (2, 1024)
        init = lambda k, shape: jax.random.normal(k, shape, jnp.float32) * 0.02
        return {'x': jax.random.normal(ks[0], (B, N, DIM), jnp.float32), 'Wqkv': init(ks[1], (DEPTH, DIM, 3 * INNER)), 'q_scale': jnp.ones((DEPTH, DIM_HEAD), jnp.float32), 'k_scale': jnp.ones((DEPTH, DIM_HEAD), jnp.float32), 'Wo': init(ks[2], (DEPTH, INNER, DIM)), 'ln_g': jnp.ones((DEPTH, DIM), jnp.float32), 'ln_b': jnp.zeros((DEPTH, DIM), jnp.float32), 'W1': init(ks[3], (DEPTH, DIM, 2 * DIM_INNER)), 'b1': jnp.zeros((DEPTH, 2 * DIM_INNER), jnp.float32), 'W2': init(ks[4], (DEPTH, DIM_INNER, DIM)), 'b2': jnp.zeros((DEPTH, DIM), jnp.float32)}
    _L0_ffn_all = _L0_ffn_setup()
    _L0_ffn_in = {k: v for k, v in _L0_ffn_all.items() if k in ('Wqkv', 'q_scale', 'k_scale', 'Wo', 'ln_g', 'ln_b', 'W1', 'b1', 'W2', 'b2')}
    del _L0_ffn_all
    return {'x': x, 'ctx_512': ctx_512, 'L0_xattn_Wq': _L0_xattn_in['Wq'], 'L0_xattn_bq': _L0_xattn_in['bq'], 'L0_xattn_Wk': _L0_xattn_in['Wk'], 'L0_xattn_bk': _L0_xattn_in['bk'], 'L0_xattn_Wv': _L0_xattn_in['Wv'], 'L0_xattn_bv': _L0_xattn_in['bv'], 'L0_xattn_Wo': _L0_xattn_in['Wo'], 'L0_xattn_bo': _L0_xattn_in['bo'], 'L0_attn_wq': _L0_attn_in['wq'], 'L0_attn_wk_down': _L0_attn_in['wk_down'], 'L0_attn_wv_down': _L0_attn_in['wv_down'], 'L0_attn_wk_up': _L0_attn_in['wk_up'], 'L0_attn_wv_up': _L0_attn_in['wv_up'], 'L0_attn_wo': _L0_attn_in['wo'], 'L0_ffn_Wqkv': _L0_ffn_in['Wqkv'], 'L0_ffn_q_scale': _L0_ffn_in['q_scale'], 'L0_ffn_k_scale': _L0_ffn_in['k_scale'], 'L0_ffn_Wo': _L0_ffn_in['Wo'], 'L0_ffn_ln_g': _L0_ffn_in['ln_g'], 'L0_ffn_ln_b': _L0_ffn_in['ln_b'], 'L0_ffn_W1': _L0_ffn_in['W1'], 'L0_ffn_b1': _L0_ffn_in['b1'], 'L0_ffn_W2': _L0_ffn_in['W2'], 'L0_ffn_b2': _L0_ffn_in['b2']}

def reference(x, ctx_512, L0_xattn_Wq, L0_xattn_bq, L0_xattn_Wk, L0_xattn_bk, L0_xattn_Wv, L0_xattn_bv, L0_xattn_Wo, L0_xattn_bo, L0_attn_wq, L0_attn_wk_down, L0_attn_wv_down, L0_attn_wk_up, L0_attn_wv_up, L0_attn_wo, L0_ffn_Wqkv, L0_ffn_q_scale, L0_ffn_k_scale, L0_ffn_Wo, L0_ffn_ln_g, L0_ffn_ln_b, L0_ffn_W1, L0_ffn_b1, L0_ffn_W2, L0_ffn_b2):
    import jax
    import jax.numpy as jnp

    def _L0_xattn_ref(q, k, v, Wq, bq, Wk, bk, Wv, bv, Wo, bo):
        import jax, jax.numpy as jnp
        import numpy as np
        HEADS = 16
        D_MODEL = 512
        IMG_MODEL = 256
        D_K = D_MODEL // HEADS
        B, LQ, _ = q.shape
        LKV = k.shape[1]
        qh = (q @ Wq + bq).reshape(B, LQ, HEADS, D_K).transpose(0, 2, 1, 3)
        kh = (k @ Wk + bk).reshape(B, LKV, HEADS, D_K).transpose(0, 2, 1, 3)
        vh = (v @ Wv + bv).reshape(B, LKV, HEADS, D_K).transpose(0, 2, 1, 3)
        scale = 1.0 / np.sqrt(D_K)
        scores = jnp.einsum('bhqd,bhkd->bhqk', qh, kh) * scale
        attn = jax.nn.softmax(scores, axis=-1)
        out = jnp.einsum('bhqk,bhkd->bhqd', attn, vh)
        concat = out.transpose(0, 2, 1, 3).reshape(B, LQ, D_MODEL)
        return concat @ Wo + bo

    def _L0_attn_ref(x, wq, wk_down, wv_down, wk_up, wv_up, wo):
        import jax, jax.numpy as jnp
        import numpy as np
        D_MODEL, N_HEADS, N_KV, HEAD_DIM, D_LAT = (512, 8, 2, 128, 32)
        N_REP = N_HEADS // N_KV
        B, T = (2, 1024)
        Bq, Tq, _ = x.shape
        scale = HEAD_DIM ** (-0.5)
        q = (x @ wq).reshape(Bq, Tq, N_KV, N_REP, HEAD_DIM)
        k_lat = (x @ wk_down).reshape(Bq, Tq, N_KV, D_LAT)
        v_lat = (x @ wv_down).reshape(Bq, Tq, N_KV, D_LAT)
        k = jnp.einsum('bkhl,ld->bkhd', k_lat, wk_up)
        v = jnp.einsum('bkhl,ld->bkhd', v_lat, wv_up)
        scores = jnp.einsum('bqhrd,bkhd->bhrqk', q, k) * scale
        causal = jnp.tril(jnp.ones((Tq, Tq), dtype=bool))
        scores = jnp.where(causal, scores, jnp.finfo(scores.dtype).min)
        probs = jax.nn.softmax(scores, axis=-1)
        y = jnp.einsum('bhrqk,bkhd->bqhrd', probs, v)
        y = y.reshape(Bq, Tq, N_HEADS * HEAD_DIM)
        return y @ wo

    def _L0_ffn_ref(x, Wqkv, q_scale, k_scale, Wo, ln_g, ln_b, W1, b1, W2, b2):
        import jax, jax.numpy as jnp
        import numpy as np
        DIM = 512
        DEPTH = 6
        HEADS = 16
        DIM_HEAD = 64
        WINDOW = 128
        INNER = HEADS * DIM_HEAD
        DIM_INNER = int(DIM * 4 * 2 / 3)
        QK_SCALE = 8.0

        def shift_tokens(t):
            a, s = jnp.split(t, 2, -1)
            s = jnp.pad(s, ((0, 0), (1, 0), (0, 0)))[:, :-1]
            return jnp.concatenate([a, s], -1)

        def l2norm(t):
            return t / jnp.maximum(jnp.linalg.norm(t, axis=-1, keepdims=True), 1e-12)

        def rotate_half(x):
            x1, x2 = jnp.split(x, 2, -1)
            return jnp.concatenate([-x2, x1], -1)

        def rotary_tables(n):
            half = jnp.arange(0, DIM_HEAD, 2, dtype=jnp.float32)
            inv_freq = 1.0 / 10000.0 ** (half / DIM_HEAD)
            t = jnp.arange(n, dtype=jnp.float32)
            freqs = t[:, None] * inv_freq[None, :]
            freqs = jnp.concatenate([freqs, freqs], -1)
            base_scale = (half + 0.4 * DIM_HEAD) / (1.4 * DIM_HEAD)
            power = (t - n // 2) / (WINDOW // 2)
            scale = base_scale[None, :] ** power[:, None]
            scale = jnp.concatenate([scale, scale], -1)
            return (freqs, scale)

        def local_attention(q, k, v):
            b, h, n, d = q.shape
            w = WINDOW
            nw = n // w
            bq = q.reshape(b, h, nw, w, d)
            bk = k.reshape(b, h, nw, w, d)
            bv = v.reshape(b, h, nw, w, d)

            def look(t):
                p = jnp.pad(t, ((0, 0), (0, 0), (1, 0), (0, 0), (0, 0)))
                return jnp.concatenate([p[:, :, :nw], p[:, :, 1:]], axis=3)
            bk2, bv2 = (look(bk), look(bv))
            seq = jnp.arange(n).reshape(nw, w)
            seq_p = jnp.pad(seq, ((1, 0), (0, 0)), constant_values=-1)
            jt = jnp.concatenate([seq_p[:nw], seq_p[1:]], axis=1)
            it = seq[:, :, None]
            jb = jt[:, None, :]
            mask = (it < jb) | (it > jb + w) | (jb == -1)
            sim = jnp.einsum('bhwie,bhwje->bhwij', bq, bk2) * QK_SCALE
            sim = jnp.where(mask, -jnp.finfo(sim.dtype).max, sim)
            attn = jax.nn.softmax(sim, -1)
            out = jnp.einsum('bhwij,bhwje->bhwie', attn, bv2)
            return out.reshape(b, h, n, d)

        def attn_layer(x, Wqkv, qs, ksc, Wo):
            b, n, _ = x.shape
            qkv = x @ Wqkv
            q, k, v = jnp.split(qkv, 3, -1)
            sh = lambda t: t.reshape(b, n, HEADS, DIM_HEAD).transpose(0, 2, 1, 3)
            q, k, v = (sh(q), sh(k), sh(v))
            q = l2norm(q) * qs
            k = l2norm(k) * ksc
            freqs, scale = rotary_tables(n)
            cos, sin = (jnp.cos(freqs), jnp.sin(freqs))
            q = q * cos * scale + rotate_half(q) * sin * scale
            inv = 1.0 / scale
            k = k * cos * inv + rotate_half(k) * sin * inv
            out = local_attention(q, k, v)
            out = out.transpose(0, 2, 1, 3).reshape(b, n, INNER)
            return out @ Wo

        def ffn_layer(x, g, bln, W1, b1, W2, b2):
            mu = x.mean(-1, keepdims=True)
            var = ((x - mu) ** 2).mean(-1, keepdims=True)
            xn = (x - mu) / jnp.sqrt(var + 1e-05) * g + bln
            hg = xn @ W1 + b1
            a, gate = jnp.split(hg, 2, -1)
            return a * jax.nn.gelu(gate, approximate=False) @ W2 + b2
        for i in range(DEPTH):
            x = attn_layer(shift_tokens(x), Wqkv[i], q_scale[i], k_scale[i], Wo[i]) + x
            x = ffn_layer(shift_tokens(x), ln_g[i], ln_b[i], W1[i], b1[i], W2[i], b2[i]) + x
        return x
    x = x + _L0_xattn_ref(_layernorm(x, axis=-1), ctx_512, ctx_512, L0_xattn_Wq, L0_xattn_bq, L0_xattn_Wk, L0_xattn_bk, L0_xattn_Wv, L0_xattn_bv, L0_xattn_Wo, L0_xattn_bo)
    x = x + _L0_attn_ref(_layernorm(x, axis=-1), L0_attn_wq, L0_attn_wk_down, L0_attn_wv_down, L0_attn_wk_up, L0_attn_wv_up, L0_attn_wo)
    x = x + _L0_ffn_ref(_layernorm(x, axis=-1), L0_ffn_Wqkv, L0_ffn_q_scale, L0_ffn_k_scale, L0_ffn_Wo, L0_ffn_ln_g, L0_ffn_ln_b, L0_ffn_W1, L0_ffn_b1, L0_ffn_W2, L0_ffn_b2)
    return x

_drawn_inputs = setup_inputs


def setup_inputs(seed=0):
    import zlib

    import numpy as np

    out = dict(_drawn_inputs(seed))
    spreads = {'L0_xattn_bq': (0.0, 0.379),
     'L0_xattn_bk': (0.0, 0.8),
     'L0_xattn_bv': (0.0, 0.1),
     'L0_xattn_bo': (0.0, 0.1),
     'L0_ffn_q_scale': (1.0, 0.6),
     'L0_ffn_k_scale': (1.0, 0.6),
     'L0_ffn_ln_g': (1.0, 0.2),
     'L0_ffn_ln_b': (0.0, 0.53),
     'L0_ffn_b1': (0.0, 0.1),
     'L0_ffn_b2': (0.0, 0.1)}
    factors = {}
    for name, (base, spread) in spreads.items():
        noise = np.random.default_rng([zlib.crc32(name.encode()), seed]).standard_normal(out[name].shape)
        drawn = base * np.exp(spread * noise) if base else spread * noise
        out[name] = jnp.asarray(drawn.astype(out[name].dtype))
    for name, factor in factors.items():
        out[name] = (out[name] * factor).astype(out[name].dtype)
    return out
```

```python
from contextlib import ExitStack

import numpy as np

import concourse.bass as bass
from concourse import mybir

P = 128
NB = 4
F32 = mybir.dt.float32
F32R = mybir.dt.float32r
ALU = mybir.AluOpType
ACT = mybir.ActivationFunctionType
AX = mybir.AxisListType
MASKED = -1e37
LN_SHIFT = 2.0 ** 20
LN_EXP_SET = "natural_log_exp_and_others"


class Signal:

    def __init__(self, sem, per, first=0):
        self.sem, self.per, self.first = sem, per, first

    def at(self, turn, n):
        return turn * self.per + (self.first + n)


def rotary_factors():
    half = np.arange(0, 64, 2, dtype=np.float32)
    inv_freq = (1.0 / 10000.0 ** (half / 64)).astype(np.float32)
    t = np.arange(P, dtype=np.float32)
    freqs = t[:, None] * inv_freq[None, :]
    base = (half + np.float32(0.4 * 64)) / np.float32(1.4 * 64)
    scale = base[None, :] ** ((t - P // 2) / np.float32(64))[:, None]
    cos, sin = np.cos(freqs), np.sin(freqs)
    tabs = []
    for s in (scale, 1.0 / scale):
        tabs += [np.concatenate([cos * s, cos * s], -1), np.concatenate([sin * s, -sin * s], -1)]
    return np.stack(tabs, 1).astype(np.float32)


def two_attentions(nc, ctx, tabs, X, OUTER, x_dram, ctx_dram, xw, aw):
    Wq, bq, Wk, bk, Wv, bv, Wo, bo = xw
    wq, wk_down, wv_down, wk_up, wv_up, wo = aw
    S, DC = ctx_dram.shape[1:]
    D = x_dram.shape[2]
    H, DK = 16, 32
    HA, GA, DH, DL = 8, 2, 128, 32
    NC = S // 512
    KT = D // P
    SCALE, SCALE_A = float(DK) ** -0.5, float(DH) ** -0.5

    ident, shiftm, maskadd, _ = tabs

    def sb(name, shape, dt=F32):
        return ctx.enter_context(nc.sbuf_tensor(name, shape, dt))

    def ps(name, shape):
        return ctx.enter_context(nc.psum_tensor(name, shape, F32))

    def signal(name, per, first=0):
        return Signal(ctx.enter_context(nc.semaphore(name)), per, first)

    wkv_hi = sb("wkv_hi", [P, 2, 2 * D], F32R)
    wkv_lo = sb("wkv_lo", [P, 2, 2 * D], F32R)
    Wq_sb = sb("Wq_sb", [P, KT, D])
    Wo_sb = sb("Wo_sb", [P, KT, D])
    wq_sb = sb("wq_sb", [P, KT, HA * DH])
    down = sb("down", [P, KT, 2, GA * DL])
    up = sb("up", [DL, 2, DH])
    bqT = sb("bqT", [P, KT])
    bkT = sb("bkT", [P, KT])
    bvB = sb("bvB", [P, D])
    boB = sb("boB", [P, D])
    xin = sb("xin", [P, D])
    xbo = sb("xbo", [P, D])
    xn = sb("xn_a", [P, D])
    xnT = sb("xnT", [P, KT, P])
    x1 = sb("x1", [P, D])
    cin = sb("cin", [P, 2, 4, DC])
    cT_hi = sb("cT_hi", [P, 2, 2, 512], F32R)
    cT_lo = sb("cT_lo", [P, 2, 2, 512], F32R)
    wo_sb = nc.alloc_sbuf_tensor_at("wo_sb", [P, HA, D], F32, offset=nc.sbuf_base - 2 * 4 * 2 * 2 * 512)
    kT = sb("kT", [P, KT, S])
    vrow = sb("vrow_a", [P, S // P, D])
    qpad = sb("qpad", [P, H, P])
    prob = sb("prob_a", [P, 2, S])
    probT = sb("probT_a", [P, 2, 512])
    mixT = sb("mixT_a", [P, KT, P])
    recB, recT = xn, xnT.rearrange("p k t -> p (k t)")
    qT_a = prob[:, 0, 0:1024].rearrange("p (h t) -> p h t", h=HA)
    mixT_b = prob[:, 0, 1024:2048].rearrange("p (h t) -> p h t", h=HA)
    prob_b = prob[:, 1, 0:1024].rearrange("p (h t) -> p h t", h=HA)
    probT_b = prob[:, 1, 1024:2048].rearrange("p (h t) -> p h t", h=HA)
    lat = sb("lat", [DL, 4, P])
    kv_a = sb("kv_a", [P, 4, P])
    rmax4 = sb("rmax4", [P, 4])
    rmax = sb("rmax", [P, 8])
    nmax = sb("nmax", [P, 8])
    sums = sb("sums", [P, H])
    rsum = sb("rsum", [P, H])
    stats = sb("stats_a", [P, 6])
    meanvar = sb("meanvar_a", [P, 2])
    halfvar = sb("halfvar_a", [P, 1])
    lnbuf = sb("lnbuf_a", [P, 1])
    rstd = sb("rstd_a", [P, 1])
    step_tmp = sb("step_tmp_a", [P, 1])

    score = ps("score_a", [P, 4, 512])
    turnb = ps("turn_a", [P, 2, 512])
    outb = ps("out_a", [P, 512])
    miscb = ps("misc_a", [P, 512])

    weights_loaded = signal("weights_loaded", 0)
    wo_loaded = signal("wo_loaded", 16)
    kv_loaded = signal("kv_loaded", 0)
    wkv_hi_ready = signal("wkv_hi_ready", 0)
    wkv_ready = signal("wkv_ready", 0)
    cleared = signal("cleared", 0)
    x_loaded = signal("x_loaded", 16)
    c_loaded = [signal(f"c_loaded{i}", 16 * NC // 2) for i in range(2)]
    stats_ready = signal("stats_ready_a", 3 * 3)
    stats_seen = signal("stats_seen_a", 3)
    logs_ready = signal("logs_ready_a", 3)
    rstd_ready = signal("rstd_ready_a", 3)
    newton_step = signal("newton_step_a", 3 * 3)
    xn_ready = signal("xn_ready_a", 2)
    xnT_done = signal("xnT_done", 2)
    xnT_ready = signal("xnT_ready", 2)
    q_done = signal("q_done", 1)
    q_ready = signal("q_ready", 1)
    cT_done = signal("cT_done", NC, 1)
    chi_ready = signal("chi_ready", NC)
    clo_ready = signal("clo_ready", NC)
    kv_done = signal("kv_done", 8 * NC)
    k_ready = signal("k_ready", 4 * NC)
    v_ready = signal("v_ready_a", 4 * NC)
    s_done = signal("s_done", 4 * H)
    chunkmax_ready = signal("chunkmax_ready", 4 * H)
    max_ready = signal("max_ready_a", H)
    nmax_ready = signal("nmax_ready", H)
    p_ready = signal("p_ready", H)
    pT_done = signal("pT_done", 4 * H)
    pT_act = signal("pT_act", 2 * H)
    pT_dve = signal("pT_dve", 2 * H)
    pv_done = signal("pv_done", H)
    rec_ready = signal("rec_ready", 2)
    recT_done = signal("recT_done", 1)
    recT_ready = signal("recT_ready", 1)
    mixT_ready = signal("mixT_ready_a", 1)
    y_done = signal("y_done", 2)
    xbo_ready = signal("xbo_ready", 1)
    x1_ready = signal("x1_ready", 1, 1)
    x2_ready = signal("x2_ready", 1, 1)
    lat_done = signal("lat_done", 2)
    qa_ready = signal("qa_ready", 1)
    lat_ready = signal("lat_ready", 1)
    kva_done = signal("kva_done", 1)
    kva_ready = signal("kva_ready", 1)
    sb_done = signal("scores_b_done", 1)
    masked = signal("masked_b", 3)
    pb_ready = signal("probs_b_ready", 1)
    pb_normed = signal("probs_b_normed", 2)
    pTb_done = signal("pTb_done", 2)
    pTb_act = signal("pTb_act", 1)
    pTb_dve = signal("pTb_dve", 1)
    ob_done = signal("ob_done", 2)
    ob_act = signal("ob_act", 1)
    ob_dve = signal("ob_dve", 1)
    x_out = signal("x_out", 1, 1)

    block = ctx.enter_context(nc.Block())

    @block.sync
    def _(sp):
        raw = prob[:, 0].rearrange("p (t n) -> p t n", t=2)
        sp.dma_start(raw[:, :, 0:D], Wk.rearrange("(t p) n -> p t n", p=P)).then_inc(kv_loaded.sem, 16)
        sp.dma_start(raw[:, :, D:2 * D], Wv.rearrange("(t p) n -> p t n", p=P)).then_inc(kv_loaded.sem, 16)
        sem = weights_loaded.sem

        def load_context(b, c):
            src = ctx_dram[bass.ds(b, 1)].rearrange("o (c t p) d -> p (o c) t d", p=P, t=4)
            sp.dma_start(cin[:, c % 2], src[:, c]).then_inc(c_loaded[c % 2].sem, 16)

        sp.dma_start(xin[:], x_dram[0]).then_inc(x_loaded.sem, 16)
        load_context(0, 0)
        load_context(0, 1)
        sp.dma_start(Wq_sb[:], Wq.rearrange("(t p) n -> p t n", p=P)).then_inc(sem, 16)
        for row, bias in ((bqT, bq), (bkT, bk)):
            sp.dma_start(row[:], bias.rearrange("(g p) -> p g", p=P), allow_slow_non_contiguous=True).then_inc(sem, 16)
        sp.dma_start(bvB[:], bv.rearrange("(o n) -> o n", o=1).to_broadcast([P, D])).then_inc(sem, 16)
        sp.dma_start(boB[:], bo.rearrange("(o n) -> o n", o=1).to_broadcast([P, D])).then_inc(sem, 16)
        sp.dma_start(Wo_sb[:], Wo.rearrange("(t p) n -> p t n", p=P)).then_inc(sem, 16)
        sp.dma_start(wq_sb[:], wq.rearrange("(t p) n -> p t n", p=P)).then_inc(sem, 16)
        for i, w in enumerate((wk_down, wv_down)):
            sp.dma_start(down[:, :, i], w.rearrange("(t p) n -> p t n", p=P)).then_inc(sem, 16)
        for i, w in enumerate((wk_up, wv_up)):
            sp.dma_start(up[:, i], w).then_inc(sem, 16)

        def batch(b, last):
            for c in range(2, NC):
                sp.wait_ge(cT_done.sem, cT_done.at(b, c - 1))
                load_context(b, c)
            sp.wait_ge(kv_done.sem, kv_done.at(b, 8 * NC))
            sp.dma_start(wo_sb[:], wo.rearrange("(t p) n -> p t n", p=P)).then_inc(wo_loaded.sem, 16)
            if not last:
                for c in range(2):
                    sp.wait_ge(cT_done.sem, cT_done.at(b, NC - 1 + c))
                    load_context(b + 1, c)
                sp.wait_ge(x1_ready.sem, x1_ready.at(b, 1))
                sp.dma_start(xin[:], x_dram[bass.ds(b + 1, 1)].rearrange("o t d -> t (o d)")).then_inc(x_loaded.sem, 16)

        with sp.Fori(0, NB - 1) as b:
            batch(b, False)
        batch(NB - 1, True)

    WEIGHTS = 16 * 11

    @block.gpsimd
    def _(pool):
        pool.wait_ge(wkv_hi_ready.sem, 1)
        nc.gpsimd.tensor_tensor(wkv_lo[:], prob[:, 0].rearrange("p (t n) -> p t n", t=2), wkv_hi[:],
                                ALU.subtract).then_inc(wkv_ready.sem, 1)
        pool.wait_ge(weights_loaded.sem, WEIGHTS)
        with pool.Fori(0, NB) as b:
            pool.wait_ge(x1_ready.sem, x1_ready.at(b, 0))
            pool.wait_ge(x_loaded.sem, x_loaded.at(b, 16))
            nc.gpsimd.tensor_tensor(xbo[:], xin[:], boB[:], ALU.add).then_inc(xbo_ready.sem, 1)

    @block.scalar
    def _(act):
        nc.scalar.preload_act_table_set(LN_EXP_SET)
        act.wait_ge(kv_loaded.sem, 32)
        nc.scalar.copy(wkv_hi[:], prob[:, 0].rearrange("p (t n) -> p t n", t=2)).then_inc(wkv_hi_ready.sem, 1)
        act.wait_ge(weights_loaded.sem, WEIGHTS)

        def inverse_deviation(b, no):
            act.wait_ge(stats_ready.sem, stats_ready.at(b, 3 * no + 3))
            nc.scalar.activation(lnbuf[:], halfvar[:], ACT.Ln, scale=-2.0).then_inc(logs_ready.sem, 1)
            act.wait_ge(logs_ready.sem, logs_ready.at(b, no + 1))
            nc.scalar.activation(rstd[:], lnbuf[:], ACT.Exp, scale=-0.5).then_inc(rstd_ready.sem, 1)

        def keep_turned_rows(b, no):
            act.wait_ge(xnT_done.sem, xnT_done.at(b, no + 1))
            nc.scalar.copy(xnT[:], miscb.rearrange("p (k t) -> p k t", k=KT)).then_inc(xnT_ready.sem, 1)

        with act.Fori(0, NB) as b:
            inverse_deviation(b, 0)
            keep_turned_rows(b, 0)

            def context_high(c):
                act.wait_ge(cT_done.sem, cT_done.at(b, c + 1))
                nc.scalar.copy(cT_hi[:, c % 2], turnb[:]).then_inc(chi_ready.sem, 1)

            context_high(0)
            context_high(1)
            for c in range(NC):
                for g in range(4):
                    act.wait_ge(kv_done.sem, kv_done.at(b, 8 * c + 2 * g + 1))
                    nc.scalar.activation(kT[:, g, 512 * c:512 * c + 512], score[:, (2 * g) % 4], ACT.Identity,
                                         bias=bkT[:, g:g + 1]).then_inc(k_ready.sem, 1)
                if c + 2 < NC:
                    context_high(c + 2)

            def keep_turned_probs(h, c, n):
                act.wait_ge(pT_done.sem, pT_done.at(b, 4 * h + c + 1))
                nc.scalar.copy(probT[:, c % 2], turnb[:, c % 2]).then_inc(pT_act.sem, 1)

            for h in range(H + 1):
                if h:
                    keep_turned_probs(h - 1, 0, 0)
                if h < H:
                    act.wait_ge(nmax_ready.sem, nmax_ready.at(b, h + 1))
                    nc.scalar.activation(prob[:, h % 2], score[:].rearrange("p c n -> p (c n)"), ACT.Exp,
                                         bias=nmax[:, 0:1], scale=SCALE,
                                         accum_out=sums[:, h:h + 1]).then_inc(p_ready.sem, 1)
                if h:
                    keep_turned_probs(h - 1, 3, 1)
            act.wait_ge(recT_done.sem, recT_done.at(b, 1))
            nc.scalar.copy(recT, miscb[:]).then_inc(recT_ready.sem, 1)

            inverse_deviation(b, 1)
            keep_turned_rows(b, 1)
            act.wait_ge(lat_done.sem, lat_done.at(b, 1))
            nc.scalar.copy(qT_a.rearrange("p h t -> p (h t)"),
                           score[:, 0:2].rearrange("p c n -> p (c n)")).then_inc(qa_ready.sem, 1)
            act.wait_ge(masked.sem, masked.at(b, 3))
            for h in range(HA):
                ins = nc.scalar.activation(prob_b[:, h], prob_b[:, h], ACT.Exp, bias=nmax[:, h:h + 1], scale=SCALE_A,
                                           accum_out=sums[:, h:h + 1])
            ins.then_inc(pb_ready.sem, 1)
            act.wait_ge(pTb_done.sem, pTb_done.at(b, 1))
            nc.scalar.copy(probT_b[:, 0:4].rearrange("p h t -> p (h t)"), turnb[:, 0]).then_inc(pTb_act.sem, 1)
            act.wait_ge(ob_done.sem, ob_done.at(b, 1))
            nc.scalar.copy(mixT_b[:, 0:4].rearrange("p h t -> p (h t)"), score[:, 2]).then_inc(ob_act.sem, 1)
            inverse_deviation(b, 2)

    @block.vector
    def _(dve):
        nc.vector.memset(qpad[:], 0.0).then_inc(cleared.sem, 1)
        nc.vector.sem_inc(x1_ready.sem, 1)
        nc.vector.sem_inc(x2_ready.sem, 1)
        nc.vector.sem_inc(x_out.sem, 1)
        dve.wait_ge(weights_loaded.sem, WEIGHTS)
        dve.wait_ge(cleared.sem, 1)

        def norm(b, no, rows, out, done):
            nc.vector.bn_stats(stats[:], rows).then_inc(stats_ready.sem, 1)
            dve.wait_ge(stats_ready.sem, stats_ready.at(b, 3 * no + 1))
            nc.vector.sem_inc(stats_seen.sem, 1)
            nc.vector.bn_aggr(meanvar[:], stats[:]).then_inc(stats_ready.sem, 1)
            dve.wait_ge(stats_ready.sem, stats_ready.at(b, 3 * no + 2))
            nc.vector.tensor_scalar(halfvar[:], meanvar[:, 1:2], 1e-5, -0.5, ALU.add,
                                    ALU.mult).then_inc(stats_ready.sem, 1)
            dve.wait_ge(rstd_ready.sem, rstd_ready.at(b, no + 1))
            nc.vector.tensor_tensor(step_tmp[:], rstd[:], rstd[:], ALU.mult).then_inc(newton_step.sem, 1)
            dve.wait_ge(newton_step.sem, newton_step.at(b, 3 * no + 1))
            nc.vector.tensor_tensor(step_tmp[:], step_tmp[:], halfvar[:], ALU.mult).then_inc(newton_step.sem, 1)
            dve.wait_ge(newton_step.sem, newton_step.at(b, 3 * no + 2))
            nc.vector.scalar_tensor_tensor(out=rstd[:], in0=step_tmp[:], scalar=1.5, in1=rstd[:], op0=ALU.add,
                                           op1=ALU.mult).then_inc(newton_step.sem, 1)
            dve.wait_ge(newton_step.sem, newton_step.at(b, 3 * no + 3))
            nc.vector.tensor_scalar(out, rows, meanvar[:, 0:1], rstd[:, 0:1], ALU.subtract,
                                    ALU.mult).then_inc(done.sem, 1)

        with dve.Fori(0, NB) as b:
            dve.wait_ge(x_loaded.sem, x_loaded.at(b, 16))
            norm(b, 0, xin[:], xn[:], xn_ready)
            dve.wait_ge(q_done.sem, q_done.at(b, 1))
            for j in range(4):
                r = slice(32 * j, 32 * j + 32)
                ins = nc.vector.tensor_tensor(qpad[r].rearrange("p (g j) t -> p j g t", j=4)[:, j],
                                              outb[r].rearrange("p (g t) -> p g t", g=4),
                                              bqT[r].unsqueeze(2).to_broadcast([32, 4, P]), ALU.add)
            ins.then_inc(q_ready.sem, 1)

            def context_low(c):
                dve.wait_ge(chi_ready.sem, chi_ready.at(b, c + 1))
                nc.vector.tensor_tensor(cT_lo[:, c % 2], turnb[:], cT_hi[:, c % 2], ALU.subtract
                                        ).then_inc(clo_ready.sem, 1)

            context_low(0)
            context_low(1)
            for c in range(NC):
                for t in range(4):
                    dve.wait_ge(kv_done.sem, kv_done.at(b, 8 * c + 2 * t + 2))
                    nc.vector.tensor_tensor(vrow[:, 4 * c + t], score[:, (2 * t + 1) % 4], bvB[:],
                                            ALU.add).then_inc(v_ready.sem, 1)
                if c + 2 < NC:
                    context_low(c + 2)
            for h in range(H + 1):
                if h < H:
                    for c in range(4):
                        dve.wait_ge(s_done.sem, s_done.at(b, 4 * h + c + 1))
                        nc.vector.tensor_reduce(rmax4[:, c:c + 1], score[:, c], AX.X,
                                                ALU.max).then_inc(chunkmax_ready.sem, 1)
                    dve.wait_ge(chunkmax_ready.sem, chunkmax_ready.at(b, 4 * h + 4))
                    nc.vector.tensor_reduce(rmax[:, 0:1], rmax4[:], AX.X, ALU.max).then_inc(max_ready.sem, 1)
                    dve.wait_ge(max_ready.sem, max_ready.at(b, h + 1))
                    nc.vector.tensor_scalar(nmax[:, 0:1], rmax[:, 0:1], -SCALE, None,
                                            ALU.mult).then_inc(nmax_ready.sem, 1)
                if h:
                    for c in (1, 2):
                        dve.wait_ge(pT_done.sem, pT_done.at(b, 4 * (h - 1) + c + 1))
                        nc.vector.tensor_copy(probT[:, c % 2], turnb[:, c % 2]).then_inc(pT_dve.sem, 1)
            dve.wait_ge(p_ready.sem, p_ready.at(b, H))
            nc.vector.reciprocal(rsum[:], sums[:]).then_inc(rec_ready.sem, 1)
            dve.wait_ge(rec_ready.sem, rec_ready.at(b, 1))
            nc.vector.tensor_copy(recB.rearrange("p (h d) -> p h d", h=H),
                                  rsum[:].unsqueeze(2).to_broadcast([P, H, DK])).then_inc(rec_ready.sem, 1)
            dve.wait_ge(recT_ready.sem, recT_ready.at(b, 1))
            dve.wait_ge(pv_done.sem, pv_done.at(b, H))
            nc.vector.tensor_tensor(mixT.rearrange("p g t -> p (g t)"), outb[:], recT,
                                    ALU.mult).then_inc(mixT_ready.sem, 1)
            dve.wait_ge(xbo_ready.sem, xbo_ready.at(b, 1))
            dve.wait_ge(y_done.sem, y_done.at(b, 1))
            nc.vector.tensor_tensor(x1[:], miscb[:], xbo[:], ALU.add).then_inc(x1_ready.sem, 1)

            dve.wait_ge(x1_ready.sem, x1_ready.at(b, 1))
            norm(b, 1, x1[:], xn[:], xn_ready)
            dve.wait_ge(lat_done.sem, lat_done.at(b, 2))
            nc.vector.tensor_copy(lat.rearrange("p i t -> p (i t)"), score[0:DL, 2]).then_inc(lat_ready.sem, 1)
            dve.wait_ge(kva_done.sem, kva_done.at(b, 1))
            nc.vector.tensor_copy(kv_a.rearrange("p i t -> p (i t)"), score[:, 3]).then_inc(kva_ready.sem, 1)
            dve.wait_ge(sb_done.sem, sb_done.at(b, 1))
            nc.vector.tensor_tensor(prob_b, score[:, 0:2].rearrange("p c (h t) -> p (c h) t", t=P),
                                    maskadd[:].unsqueeze(1).to_broadcast([P, HA, P]), ALU.add).then_inc(masked.sem, 1)
            dve.wait_ge(masked.sem, masked.at(b, 1))
            nc.vector.tensor_reduce(rmax[:], prob_b, AX.X, ALU.max).then_inc(masked.sem, 1)
            dve.wait_ge(masked.sem, masked.at(b, 2))
            nc.vector.tensor_scalar(nmax[:], rmax[:], -SCALE_A, None, ALU.mult).then_inc(masked.sem, 1)
            dve.wait_ge(pb_ready.sem, pb_ready.at(b, 1))
            nc.vector.reciprocal(rsum[:, 0:HA], sums[:, 0:HA]).then_inc(pb_normed.sem, 1)
            dve.wait_ge(pb_normed.sem, pb_normed.at(b, 1))
            nc.vector.tensor_tensor(prob_b, prob_b, rsum[:, 0:HA].unsqueeze(2).to_broadcast([P, HA, P]),
                                    ALU.mult).then_inc(pb_normed.sem, 1)
            dve.wait_ge(pTb_done.sem, pTb_done.at(b, 2))
            nc.vector.tensor_copy(probT_b[:, 4:8].rearrange("p h t -> p (h t)"), turnb[:, 1]).then_inc(pTb_dve.sem, 1)
            dve.wait_ge(ob_done.sem, ob_done.at(b, 2))
            nc.vector.tensor_copy(mixT_b[:, 4:8].rearrange("p h t -> p (h t)"), score[:, 3]).then_inc(ob_dve.sem, 1)
            dve.wait_ge(y_done.sem, y_done.at(b, 2))
            nc.vector.tensor_tensor(OUTER[:, bass.ds(b, 1)].rearrange("p o d -> p (o d)"), miscb[:], x1[:], ALU.add)
            nc.vector.tensor_tensor(x1[:], miscb[:], x1[:], ALU.add).then_inc(x2_ready.sem, 1)
            dve.wait_ge(x2_ready.sem, x2_ready.at(b, 1))
            norm(b, 2, x1[:], X[:, bass.ds(b, 1)].rearrange("p o d -> p (o d)"), x_out)
            dve.wait_ge(x_out.sem, x_out.at(b, 1))

    @block.tensor
    def _(pe):
        nc.tensor.sem_inc(cT_done.sem, 1)
        pe.wait_ge(weights_loaded.sem, WEIGHTS)
        pe.wait_ge(wkv_ready.sem, 1)
        pe.wait_ge(cleared.sem, 1)

        def three_passes(dst, lhs, rhs, first, last):
            (lh, ll), (rh, rl) = lhs, rhs
            nc.tensor.matmul(dst, lh, rh, start=first, stop=False)
            nc.tensor.matmul(dst, lh, rl, start=False, stop=False)
            return nc.tensor.matmul(dst, ll, rh, start=False, stop=last)

        def turn_rows(b, no, rows):
            pe.wait_ge(xn_ready.sem, xn_ready.at(b, no + 1))
            for k in range(KT):
                ins = nc.tensor.transpose(miscb[:, k * P:(k + 1) * P], rows[:, k * P:(k + 1) * P], ident[:])
            ins.then_inc(xnT_done.sem, 1)

        with pe.Fori(0, NB) as b:
            pe.wait_ge(x2_ready.sem, x2_ready.at(b, 0))
            turn_rows(b, 0, xn)
            pe.wait_ge(xnT_ready.sem, xnT_ready.at(b, 1))
            for g in range(4):
                for k in range(KT):
                    ins = nc.tensor.matmul(outb[:, g * P:(g + 1) * P], Wq_sb[:, k, g * P:(g + 1) * P], xnT[:, k],
                                           start=(k == 0), stop=(k == KT - 1))
            ins.then_inc(q_done.sem, 1)

            def turn_context(c):
                pe.wait_ge(c_loaded[c % 2].sem, c_loaded[c % 2].at(b, 16 * (c // 2 + 1)))
                if c:
                    pe.wait_ge(clo_ready.sem, clo_ready.at(b, c))
                for k in range(2):
                    for t in range(4):
                        ins = nc.tensor.transpose(turnb[:, k, t * P:(t + 1) * P], cin[:, c % 2, t, k * P:(k + 1) * P],
                                                  ident[:])
                ins.then_inc(cT_done.sem, 1)

            turn_context(0)
            for c in range(NC):
                if c + 1 < NC:
                    turn_context(c + 1)
                pe.wait_ge(clo_ready.sem, clo_ready.at(b, c + 1))
                parts = (cT_hi[:, c % 2], cT_lo[:, c % 2])
                for n in range(8):
                    m = 8 * c + n
                    done = k_ready if n % 2 == 0 else v_ready
                    if m >= 4:
                        pe.wait_ge(done.sem, done.at(b, (m - 4) // 2 + 1))
                    i = n // 2
                    for k in range(2):
                        if n % 2 == 0:
                            lhs = tuple(w[:, k, i * P:(i + 1) * P] for w in (wkv_hi, wkv_lo))
                            rhs = tuple(x[:, k] for x in parts)
                        else:
                            lhs = tuple(x[:, k, i * P:(i + 1) * P] for x in parts)
                            rhs = tuple(w[:, k, D:2 * D] for w in (wkv_hi, wkv_lo))
                        ins = three_passes(score[:, m % 4], lhs, rhs, k == 0, k == 1)
                    ins.then_inc(kv_done.sem, 1)

            pe.wait_ge(q_ready.sem, q_ready.at(b, 1))
            pe.wait_ge(k_ready.sem, k_ready.at(b, 4 * NC))
            pe.wait_ge(v_ready.sem, v_ready.at(b, 4 * NC))

            def weigh_values(h):
                r = 32 * (h % 4)

                def turn_probs(c):
                    if c == 2:
                        pe.wait_ge(pT_act.sem, pT_act.at(b, 2 * h + 1))
                    if c == 3:
                        pe.wait_ge(pT_dve.sem, pT_dve.at(b, 2 * h + 1))
                    if c == 0 and h:
                        pe.wait_ge(pT_dve.sem, pT_dve.at(b, 2 * h))
                    if c == 1 and h:
                        pe.wait_ge(pT_act.sem, pT_act.at(b, 2 * h))
                    for t in range(4):
                        at = (4 * c + t) * P
                        ins = nc.tensor.transpose(turnb[:, c % 2, t * P:(t + 1) * P], prob[:, h % 2, at:at + P], ident[:])
                    ins.then_inc(pT_done.sem, 1)

                def weigh(c):
                    if c in (0, 3):
                        pe.wait_ge(pT_act.sem, pT_act.at(b, 2 * h + (1 if c == 0 else 2)))
                    else:
                        pe.wait_ge(pT_dve.sem, pT_dve.at(b, 2 * h + c))
                    for t in range(4):
                        n = 4 * c + t
                        ins = nc.tensor.matmul(outb[r:r + 32, (h // 4) * P:(h // 4 + 1) * P],
                                               vrow[:, n, h * DK:(h + 1) * DK], probT[:, c % 2, t * P:(t + 1) * P],
                                               start=(n == 0), stop=(n == S // P - 1))
                    return ins

                turn_probs(0)
                turn_probs(1)
                weigh(0)
                turn_probs(2)
                weigh(1)
                turn_probs(3)
                weigh(2)
                weigh(3).then_inc(pv_done.sem, 1)

            for h in range(H):
                if h:
                    pe.wait_ge(p_ready.sem, p_ready.at(b, h))
                for c in range(4):
                    nc.tensor.matmul(score[:, c], qpad[:, h], kT[:, h // 4, 512 * c:512 * c + 512], start=True,
                                     stop=True).then_inc(s_done.sem, 1)
                if h:
                    weigh_values(h - 1)
            pe.wait_ge(p_ready.sem, p_ready.at(b, H))
            weigh_values(H - 1)
            pe.wait_ge(rec_ready.sem, rec_ready.at(b, 2))
            for g in range(4):
                ins = nc.tensor.transpose(miscb[:, g * P:(g + 1) * P], recB[:, g * P:(g + 1) * P], ident[:])
            ins.then_inc(recT_done.sem, 1)
            pe.wait_ge(mixT_ready.sem, mixT_ready.at(b, 1))
            for g in range(KT):
                ins = nc.tensor.matmul(miscb[:], mixT[:, g], Wo_sb[:, g], start=(g == 0), stop=(g == KT - 1))
            ins.then_inc(y_done.sem, 1)

            turn_rows(b, 1, xn)
            pe.wait_ge(xnT_ready.sem, xnT_ready.at(b, 2))
            for h in range(HA):
                for k in range(KT):
                    ins = nc.tensor.matmul(score[:, h // 4, (h % 4) * P:(h % 4 + 1) * P], wq_sb[:, k, h * DH:(h + 1) * DH],
                                           xnT[:, k], start=(k == 0), stop=(k == KT - 1))
            ins.then_inc(lat_done.sem, 1)
            for i in range(2 * GA):
                for k in range(KT):
                    ins = nc.tensor.matmul(score[0:DL, 2, i * P:(i + 1) * P],
                                           down[:, k, i // 2, (i % 2) * DL:(i % 2 + 1) * DL], xnT[:, k],
                                           start=(k == 0), stop=(k == KT - 1))
            ins.then_inc(lat_done.sem, 1)
            pe.wait_ge(lat_ready.sem, lat_ready.at(b, 1))
            for g in range(GA):
                nc.tensor.matmul(score[:, 3, g * P:(g + 1) * P], up[:, 0], lat[:, g], start=True, stop=True)
            for g in range(GA):
                ins = nc.tensor.matmul(score[:, 3, (GA + g) * P:(GA + g + 1) * P], lat[:, GA + g], up[:, 1], start=True,
                                       stop=True)
            ins.then_inc(kva_done.sem, 1)
            pe.wait_ge(kva_ready.sem, kva_ready.at(b, 1))
            pe.wait_ge(qa_ready.sem, qa_ready.at(b, 1))
            for h in range(HA):
                ins = nc.tensor.matmul(score[:, h // 4, (h % 4) * P:(h % 4 + 1) * P], qT_a[:, h], kv_a[:, h // 4],
                                       start=True, stop=True)
            ins.then_inc(sb_done.sem, 1)
            pe.wait_ge(pb_normed.sem, pb_normed.at(b, 2))
            for h in range(HA):
                ins = nc.tensor.transpose(turnb[:, h // 4, (h % 4) * P:(h % 4 + 1) * P], prob_b[:, h], ident[:])
                if h % 4 == 3:
                    ins.then_inc(pTb_done.sem, 1)
            for g in range(GA):
                if g == 0:
                    pe.wait_ge(pTb_act.sem, pTb_act.at(b, 1))
                else:
                    pe.wait_ge(pTb_dve.sem, pTb_dve.at(b, 1))
                nc.tensor.matmul(score[:, 2 + g], kv_a[:, GA + g],
                                 probT_b[:, 4 * g:4 * g + 4].rearrange("p h t -> p (h t)"), start=True,
                                 stop=True).then_inc(ob_done.sem, 1)
            for h in range(HA):
                if h == 0:
                    pe.wait_ge(wo_loaded.sem, wo_loaded.at(b, 16))
                    pe.wait_ge(ob_act.sem, ob_act.at(b, 1))
                if h == 4:
                    pe.wait_ge(ob_dve.sem, ob_dve.at(b, 1))
                ins = nc.tensor.matmul(miscb[:], mixT_b[:, h], wo_sb[:, h], start=(h == 0), stop=(h == HA - 1))
            ins.then_inc(y_done.sem, 1)


def local_transformer(nc, ctx, tabs, X, OUTER, out_dram, w):
    Wqkv, q_scale, k_scale, Wo, ln_g, ln_b, W1, b1, W2, b2 = w
    DEPTH = Wqkv.shape[0]
    HEADS_HALF, DH = 8, 64
    INNER2 = W2.shape[1]
    FT = (INNER2 + P - 1) // P
    FTAIL = INNER2 - (FT - 1) * P
    QK_SCALE = 8.0

    chunk_names = [("qkv", 0, 0), ("qkv", 1, 0), ("qkv", 2, 0), ("qkv", 0, 1), ("qkv", 1, 1), ("qkv", 2, 1),
                   ("wo", 0), ("wo", 1)] + [("w1", c) for c in range(6)] + [("w2", c) for c in range(4)]
    NCH = len(chunk_names)
    C_Q0, C_WO, C_W1, C_W2 = 0, 6, 8, 14
    QKV_UNITS = [(0, b) for b in range(NB)] + [(1, b) for b in range(NB)] + [(2, b) for b in range(NB)]
    QKV_UNITS += [(c, b) for b in range(NB) for c in (3, 4)] + [(5, b) for b in range(NB)]
    WO_UNITS = [(C_WO + h, b) for h in range(2) for b in range(NB)]
    NQ, NO = len(QKV_UNITS), len(WO_UNITS)
    U_W1 = NQ + NO
    U_W2 = U_W1 + 2 * FT
    NU = U_W2 + NB
    rot_units = [u for u in range(NQ) if QKV_UNITS[u][0] % 3 != 2]
    rot_no = {u: n for n, u in enumerate(rot_units)}
    NROT = len(rot_units)
    v_units = [u for u in range(NQ) if u not in rot_no]
    v_no = {u: n for n, u in enumerate(v_units)}
    steps = [("turn_x", b) for b in range(NB)]
    rot_wait = {"norm": None, "add": None}

    def emit_unit(u):
        steps.append(("products", u))
        if rot_wait["norm"] is not None:
            steps.append(("normalise", rot_wait["norm"]))
        if rot_wait["add"] is not None:
            steps.append(("rotate", rot_wait["add"]))
        rot_wait["add"] = rot_wait["norm"]
        rot_wait["norm"] = u if u in rot_no else None
        steps.append(("empty", u))

    for u in range(12):
        emit_unit(u)
    uq = iter(range(12, NQ))
    for a in range(NB):
        steps.append(("turn_qk", a))
        emit_unit(next(uq))
        steps.append(("scores", a))
        emit_unit(next(uq))
        if a:
            steps.append(("values", a - 1))
    for a in range(NB, 2 * NB):
        if a == NB:
            emit_unit(next(uq))
            steps.append(("turn_qk", a))
        else:
            steps.append(("turn_qk", a))
            emit_unit(next(uq))
        steps.append(("scores", a))
        steps.append(("values", a - 1))
    for b in range(3):
        emit_unit(NQ + b)
    steps.append(("values", 2 * NB - 1))
    emit_unit(NQ + 3)
    emit_unit(NQ + 4)
    emit_unit(NQ + 5)
    steps.append(("shift", 0))
    emit_unit(NQ + 6)
    steps.append(("shift", 1))
    emit_unit(NQ + 7)
    steps.append(("turn_n", 0))
    steps.append(("shift", 2))
    steps.append(("turn_n", 1))
    steps.append(("shift", 3))
    steps.append(("turn_n", 2))
    steps.append(("turn_n", 3))
    for f in range(FT):
        steps.append(("gate", f))
        steps.append(("value", f))
    steps.append(("last_split", 0))
    for c in range(4):
        for b in range(NB):
            steps.append(("down", c, b))
    for b in range(NB):
        steps.append(("add_down", b))

    first_use, last_use = {}, {}

    def chunks_of(step):
        if step[0] == "products":
            u = step[1]
            return QKV_UNITS[u][0] if u < NQ else WO_UNITS[u - NQ][0]
        if step[0] == "gate" or step[0] == "value":
            return C_W1 + step[1] // 2
        if step[0] == "down":
            return C_W2 + step[1]
        return None

    for n, s in enumerate(steps):
        c = chunks_of(s)
        if c is not None:
            first_use.setdefault(c, n)
            last_use[c] = n
    split_at = {}
    for c in range(NCH):
        uses = [n for n, s in enumerate(steps) if chunks_of(s) == c]
        uses = [n for n in uses if n > last_use.get(c - 1, -1)] or [last_use[c]]
        for t in range(4):
            split_at.setdefault(uses[min(len(uses) - 1, t * len(uses) // 4)], []).append((c + 2, t))

    turns = []
    for s in steps:
        if s[0] == "turn_x" or s[0] == "turn_n":
            turns.append((s[0], s[1], 0))
        elif s[0] == "turn_qk" or s[0] == "values":
            turns += [(s[0], s[1], 0), (s[0], s[1], 1)]
    turn_no = {t: n for n, t in enumerate(turns)}
    NTURN = len(turns)
    turn_act = {}
    turn_dve = {}
    for n, t in enumerate(turns):
        if t[0] == "turn_qk" and t[2] == 1 or t[0] == "values" and t[2] == 0:
            turn_act[n] = len(turn_act)
        else:
            turn_dve[n] = len(turn_dve)
    assert all(n % 2 == t[2] for n, t in enumerate(turns) if t[0] in ("turn_qk", "values")) and NTURN % 2 == 0
    mixed = [s for s in steps if s[0] in ("values", "shift")]
    mix_no = {s: n for n, s in enumerate(mixed)}
    NMIX = len(mixed)

    def sb(name, shape, dt=F32):
        return ctx.enter_context(nc.sbuf_tensor(name, shape, dt))

    def ps(name, shape):
        return ctx.enter_context(nc.psum_tensor(name, shape, F32))

    def signal(name, per, first=0):
        return Signal(ctx.enter_context(nc.semaphore(name)), per, first)

    ident, shiftm, maskadd, rotary_dram = tabs

    raw = [sb(f"raw{i}", [P, 4, 512]) for i in range(2)]
    whi = [sb(f"whi{i}", [P, 4, 512], F32R) for i in range(3)]
    wlo = [sb(f"wlo{i}", [P, 4, 512], F32R) for i in range(3)]
    xt_hi = sb("xt_hi", [P, 4, NB * P], F32R)
    xt_lo = sb("xt_lo", [P, 4, NB * P], F32R)
    HID = FT * 512
    QKVW, ATW = 3 * NB * 512, 2 * 8 * 128 * 3 + 2 * 512
    region = sb("region", [P, QKVW + ATW])
    region_address = nc.sbuf_base - 4 * (QKVW + ATW)
    qrow = region[:, 0:NB * 512].rearrange("p (b n) -> p b n", b=NB)
    krow = region[:, NB * 512:2 * NB * 512].rearrange("p (b n) -> p b n", b=NB)
    vrow = region[:, 2 * NB * 512:3 * NB * 512].rearrange("p (b n) -> p b n", b=NB)
    at = QKVW
    qT = region[:, at:at + 1024].rearrange("p (s h t) -> p s h t", s=2, h=4)
    at += 1024
    prob = region[:, at:at + 2048].rearrange("p (s h t) -> p s h t", s=2, h=8)
    at += 2048
    probT = region[:, at:at + 2048].rearrange("p (s h t) -> p s h t", s=2, h=8)
    at += 2048
    assert at >= 2 * HID
    kD = region[:, at:at + 2048].rearrange("p (s h e t) -> p s h e t", s=2, h=4, e=2)
    where = region_address
    hid_hi = nc.alloc_sbuf_tensor_at("hid_hi", [P, FT, 512], F32R, offset=where)
    hid_lo = nc.alloc_sbuf_tensor_at("hid_lo", [P, FT, 512], F32R, offset=where + 4 * HID)
    mixT_hi = sb("mixT_hi", [P, 8, NB * P], F32R)
    mixT_lo = sb("mixT_lo", [P, 8, NB * P], F32R)
    sq = sb("sq", [P, 512])
    wide_a = sb("wide_a", [P, 2, 512])
    wide_b = sb("wide_b", [P, 2, 512])
    qn, xn, hfull = wide_a, wide_a, wide_a
    turned_half, gate_out = wide_b, wide_b
    ss = sb("ss", [P, 2, 8])
    rn = sb("rn", [P, 2, 8])
    negmax = sb("negmax", [P, 2, 8])
    rowmax = sb("rowmax", [P, 8])
    psums = sb("psums", [P, 2, 8])
    rsums = sb("rsums", [P, 8])
    stats = sb("stats", [P, 12])
    meanvar = sb("meanvar", [P, 2, 2])
    rstd = sb("rstd", [P, 2])
    stats_seen = signal("stats_seen", NB)
    halfvar = sb("halfvar", [P, 2])
    lnbuf = sb("lnbuf", [P, 9])
    step_tmp = sb("step_tmp", [P, 8])
    half_log = sb("half_log", [P, 1])
    base_tab = sb("base_tab", [P, 4, DH])
    scales = sb("scales", [P, 2, DEPTH, DH])
    cur_tab = sb("cur_tab", [P, 4, DH])
    gB = sb("gB", [P, 512])
    bB = sb("bB", [P, 512])
    b2B = sb("b2B", [P, 512])
    b1T = sb("b1T", [P, 2 * FT])

    proj = [ps(f"proj{i}", [P, 512]) for i in range(3)]
    turnb = [ps(f"turnb{i}", [P, 512]) for i in range(2)]
    score = ps("score", [P, 8, P])
    mix = ps("mix", [P, 512])

    raw_loaded = [signal(f"raw_loaded{i}", 0) for i in range(2)]
    tables_loaded = signal("tables_loaded", 0)
    layer_loaded = signal("layer_loaded", 0)
    hi_ready = signal("hi_ready", NCH, 2)
    lo_ready = signal("lo_ready", NCH, 2)
    down_used = signal("down_used", 3, 3)
    proj_done = signal("proj_done", NU, 1)
    v_ready = signal("v_ready", 2 * NB)
    x_added = signal("x_added", NO)
    gate_read = signal("gate_read", FT)
    turned = signal("turned", NTURN)
    turn_read_act = signal("turn_read_act", len(turn_act), 2)
    turn_read_dve = signal("turn_read_dve", len(turn_dve), 2)
    xhi_ready = signal("xhi_ready", 2 * NB)
    squared = signal("squared", NROT)
    sumsq_ready = signal("sumsq_ready", 2 * NROT, 2)
    logs_ready = signal("logs_ready", NROT + NB)
    newton_step = signal("newton_step", 3 * (NROT + NB))
    rnorm_ready = signal("rnorm_ready", NROT)
    normed = signal("normed", NROT)
    parts_rotated = signal("parts_rotated", NROT, 2)
    rotated = signal("rotated", NROT, 2)
    tabs_ready = signal("tabs_ready", 2)
    scored = signal("scored", 8)
    scores_read = signal("scores_read", 8, 1)
    max_ready = signal("max_ready", 8)
    negmax_ready = signal("negmax_ready", 8)
    probs_ready = signal("probs_ready", 8)
    recip_ready = signal("recip_ready", 8)
    probs_normed = signal("probs_normed", 8)
    mix_done = signal("mix_done", NMIX)
    mixlo_ready = signal("mixlo_ready", 2 * NB)
    mixhi_ready = signal("mixhi_ready", 8)
    stats_ready = signal("stats_ready", 3 * NB)
    rstd_ready = signal("rstd_ready", NB)
    ln_normed = signal("ln_normed", NB)
    ln_scaled = signal("ln_scaled", NB)
    ln_ready = signal("ln_ready", NB)
    x_biased = signal("x_biased", NB)
    hidden_full = signal("hidden_full", FT)
    hidhi_ready = signal("hidhi_ready", FT)
    hidlo_ready = signal("hidlo_ready", FT)
    x_new = signal("x_new", NB, NB)
    zero_ready = signal("zero_ready", 0)
    sum_ready = signal("sum_ready", 0)
    stored = signal("stored", 0)

    dmas_of = [2 if name[0] == "w1" or name == ("w2", 3) else 1 for name in chunk_names]
    slot_total = [16 * sum(d for c, d in enumerate(dmas_of) if c % 2 == s) for s in range(2)]
    for s in range(2):
        raw_loaded[s].per = slot_total[s]

    def landed(c):
        return 16 * sum(d for k, d in enumerate(dmas_of[:c + 1]) if k % 2 == c % 2)

    LAYER_DMAS = 7
    layer_loaded.per = 16 * LAYER_DMAS

    def piece(buf, c, t):
        name = chunk_names[c]
        if name == ("w1", 5):
            return buf[:, t].rearrange("p (g n) -> p g n", g=2)[:, :, 0:FTAIL]
        if name[0] == "w2" and t == 3 or name == ("w2", 3) and t >= 2:
            return None
        if name == ("w2", 3) and t == 1:
            return buf[0:FTAIL, t, :]
        return buf[:, t, :]

    def npieces(c):
        return sum(piece(raw[0], c, t) is not None for t in range(4))

    def row(ap, l):
        return ap[bass.ds(l, 1)]

    block = ctx.enter_context(nc.Block())

    @block.sync
    def _(sp):
        sp.dma_start(base_tab[:], rotary_dram).then_inc(tables_loaded.sem, 16)
        sp.dma_start(scales[:, 0], q_scale.rearrange("(o l) d -> o l d", o=1).to_broadcast([P, DEPTH, DH])
                     ).then_inc(tables_loaded.sem, 16)
        sp.dma_start(scales[:, 1], k_scale.rearrange("(o l) d -> o l d", o=1).to_broadcast([P, DEPTH, DH])
                     ).then_inc(tables_loaded.sem, 16)

        def load(l, c):
            sp.wait_ge(lo_ready.sem, lo_ready.at(l, c - 1))
            name, buf, sem = chunk_names[c], raw[c % 2], raw_loaded[c % 2].sem
            if name[0] == "qkv":
                col = name[1] * 1024 + name[2] * 512
                src = row(Wqkv, l).rearrange("o (t p) n -> p (o t) n", p=P)[:, :, col:col + 512]
                sp.dma_start(buf[:], src).then_inc(sem, 16)
            elif name[0] == "wo":
                src = row(Wo, l).rearrange("o (t p) n -> p (o t) n", p=P)[:, 4 * name[1]:4 * name[1] + 4]
                sp.dma_start(buf[:], src).then_inc(sem, 16)
            elif name[0] == "w1":
                n = 256 if name[1] < 5 else FTAIL
                src = row(W1, l).rearrange("o (t p) n -> p (o t) n", p=P)
                for g, base in enumerate((INNER2, 0)):
                    col = base + 256 * name[1]
                    sp.dma_start(buf[:, :, 256 * g:256 * g + n], src[:, :, col:col + n]).then_inc(sem, 16)
            else:
                r0 = 3 * P * name[1]
                full = 3 if name[1] < 3 else 1
                src = row(W2, l).rearrange("o r n -> (o r) n")
                sp.dma_start(buf[:, 0:full], src[r0:r0 + full * P].rearrange("(t p) n -> p t n", p=P)).then_inc(sem, 16)
                if name[1] == 3:
                    sp.dma_start(buf[0:FTAIL, 1], src[r0 + P:r0 + P + FTAIL]).then_inc(sem, 16)

        def load_layer(l):
            sp.wait_ge(x_new.sem, x_new.at(l, 0))
            sem = layer_loaded.sem
            sp.dma_start(gB[:], row(ln_g, l).to_broadcast([P, 512])).then_inc(sem, 16)
            sp.dma_start(bB[:], row(ln_b, l).to_broadcast([P, 512])).then_inc(sem, 16)
            sp.dma_start(b2B[:], row(b2, l).to_broadcast([P, 512])).then_inc(sem, 16)
            bias = row(b1, l).rearrange("o n -> (o n)")
            for g, base in enumerate((INNER2, 0)):
                n = (FT - 1) * P
                sp.dma_start(b1T[:, g * FT:g * FT + FT - 1],
                             bias[base:base + n].rearrange("(f p) -> p f", p=P),
                             allow_slow_non_contiguous=True).then_inc(sem, 16)
                sp.dma_start(b1T[0:FTAIL, g * FT + FT - 1:g * FT + FT],
                             bias[base + n:base + n + FTAIL].rearrange("(p f) -> p f", f=1),
                             allow_slow_non_contiguous=True).then_inc(sem, 16)

        load(0, 0)
        load(0, 1)

        def layer(l, last):
            for c in range(2, NCH):
                if c == 4:
                    load_layer(l)
                load(l, c)
            if not last:
                load(l + 1, 0)
                load(l + 1, 1)

        with sp.Fori(0, DEPTH - 1) as l:
            layer(l, False)
        layer(DEPTH - 1, True)
        for b in range(NB):
            sp.wait_ge(sum_ready.sem, b + 1)
            sp.dma_start(out_dram[b], X[:, b]).then_inc(stored.sem, 16)
        sp.wait_ge(stored.sem, 16 * NB)

    def chunk_is_used(eng, l, c):
        back = c < 0
        c = c % NCH
        if C_W2 <= c < NCH - 1:
            eng.wait_ge(down_used.sem, down_used.at(l, c - C_W2 + 1 - (down_used.per if back else 0)))
            return
        step = steps[last_use[c]]
        u = {"products": lambda: step[1], "gate": lambda: U_W1 + 2 * step[1], "value": lambda: U_W1 + 2 * step[1] + 1,
             "down": lambda: NU - 1}[step[0]]()
        eng.wait_ge(proj_done.sem, proj_done.at(l, u + 1 - (NU if back else 0)))

    def split_hi(act, l, c):
        chunk_is_used(act, l, c - 3)
        act.wait_ge(raw_loaded[c % 2].sem, raw_loaded[c % 2].at(l, landed(c)))
        n = npieces(c)
        for t in range(n):
            if chunk_names[c][0] == "w1" and chunk_names[c][1] == 5 or chunk_names[c] == ("w2", 3):
                ins = nc.scalar.copy(piece(whi[c % 3], c, t), piece(raw[c % 2], c, t))
            elif t == 0:
                ins = nc.scalar.copy(whi[c % 3][:, 0:n], raw[c % 2][:, 0:n])
        ins.then_inc(hi_ready.sem, 1)

    def split_lo(pool, l, c, t):
        if piece(raw[0], c, t) is None:
            return
        if t == 0:
            pool.wait_ge(hi_ready.sem, hi_ready.at(l, c + 1))
        ins = nc.gpsimd.tensor_tensor(piece(wlo[c % 3], c, t), piece(raw[c % 2], c, t), piece(whi[c % 3], c, t),
                                      ALU.subtract)
        if t == npieces(c) - 1:
            ins.then_inc(lo_ready.sem, 1)

    def splits(n, l, last):
        for c, t in split_at.get(n, []):
            if c < NCH:
                yield l, c, t
            elif not last:
                yield l + 1, c - NCH, t

    def rot_buf(u):
        c, b = QKV_UNITS[u]
        return (qrow, krow)[c % 3][:, b]

    @block.scalar
    def _(act):
        nc.scalar.sem_inc(hi_ready.sem, 2)
        nc.scalar.sem_inc(turn_read_act.sem, 2)
        act.wait_ge(zero_ready.sem, 1)
        split_hi(act, 0, 0)
        split_hi(act, 0, 1)

        def layer(l, last):
            nc.scalar.preload_act_table_set(LN_EXP_SET)
            for n, s in enumerate(steps):
                for ll, c, t in splits(n, l, last):
                    if t == 0:
                        split_hi(act, ll, c)
                k = s[0]
                if k == "turn_x" or k == "turn_n":
                    b = s[1]
                    e = turn_no[(k, b, 0)]
                    act.wait_ge(turned.sem, turned.at(l, e + 1))
                    nc.scalar.copy(xt_hi[:, :, b * P:(b + 1) * P],
                                   turnb[e % 2].rearrange("p (k t) -> p k t", k=4)).then_inc(xhi_ready.sem, 1)
                elif k == "empty" and s[1] in rot_no:
                    u = s[1]
                    r = rot_no[u]
                    act.wait_ge(sumsq_ready.sem, sumsq_ready.at(l, 2 * r))
                    act.wait_ge(proj_done.sem, proj_done.at(l, u + 1))
                    nc.scalar.activation(sq[:], proj[u % 3][:], ACT.Square).then_inc(squared.sem, 1)
                elif k == "normalise":
                    r = rot_no[s[1]]
                    act.wait_ge(sumsq_ready.sem, sumsq_ready.at(l, 2 * r + 2))
                    nc.scalar.activation(lnbuf[:, 0:8], ss[:, r % 2], ACT.Ln,
                                         scale=-2.0 * LN_SHIFT).then_inc(logs_ready.sem, 1)
                    act.wait_ge(logs_ready.sem, logs_ready.at(l, r + 1))
                    nc.scalar.activation(rn[:, r % 2], lnbuf[:, 0:8], ACT.Exp, bias=half_log[:, 0:1],
                                         scale=-0.5).then_inc(rnorm_ready.sem, 1)
                elif k == "shift":
                    b = s[1]
                    act.wait_ge(stats_ready.sem, stats_ready.at(l, 3 * b + 3))
                    nc.scalar.activation(lnbuf[:, 8:9], halfvar[:, b % 2:b % 2 + 1], ACT.Ln,
                                         scale=-2.0).then_inc(logs_ready.sem, 1)
                    act.wait_ge(logs_ready.sem, logs_ready.at(l, NROT + b + 1))
                    nc.scalar.activation(rstd[:, b % 2:b % 2 + 1], lnbuf[:, 8:9], ACT.Exp,
                                         scale=-0.5).then_inc(rstd_ready.sem, 1)
                elif k == "turn_qk":
                    a = s[1]
                    e = turn_no[(k, a, 1)]
                    act.wait_ge(turned.sem, turned.at(l, e + 1))
                    src = turnb[1].rearrange("p (h t) -> p h t", h=4)
                    nc.scalar.copy(kD[0:64, a % 2, :, 0, :], src[0:64])
                    nc.scalar.copy(kD[64:128, a % 2, :, 1, :], src[64:128]).then_inc(turn_read_act.sem, 1)
                elif k == "scores":
                    a = s[1]
                    act.wait_ge(negmax_ready.sem, negmax_ready.at(l, a + 1))
                    for h in range(8):
                        ins = nc.scalar.activation(prob[:, a % 2, h], prob[:, a % 2, h], ACT.Exp,
                                                   bias=negmax[:, a % 2, h:h + 1], scale=QK_SCALE,
                                                   accum_out=psums[:, a % 2, h:h + 1])
                    ins.then_inc(probs_ready.sem, 1)
                elif k == "values":
                    a = s[1]
                    b, hf = a % NB, a // NB
                    e = turn_no[(k, a, 0)]
                    act.wait_ge(turned.sem, turned.at(l, e + 1))
                    nc.scalar.copy(probT[:, a % 2, 0:4],
                                   turnb[0].rearrange("p (h t) -> p h t", h=4)).then_inc(turn_read_act.sem, 1)
                    act.wait_ge(mix_done.sem, mix_done.at(l, mix_no[s] + 1))
                    nc.scalar.copy(mixT_hi[:, 4 * hf:4 * hf + 4, b * P:(b + 1) * P],
                                   mix.rearrange("p (h t) -> p h t", h=4)).then_inc(mixhi_ready.sem, 1)
                elif k == "gate":
                    f = s[1]
                    rows = P if f < FT - 1 else FTAIL
                    if f == 0:
                        act.wait_ge(layer_loaded.sem, layer_loaded.at(l, 16 * LAYER_DMAS))
                    if f >= 2:
                        act.wait_ge(hidden_full.sem, hidden_full.at(l, f - 1))
                    u = U_W1 + 2 * f
                    act.wait_ge(proj_done.sem, proj_done.at(l, u + 1))
                    nc.scalar.activation(gate_out[0:rows, f % 2], proj[u % 3][0:rows], ACT.Gelu,
                                         bias=b1T[0:rows, f:f + 1]).then_inc(gate_read.sem, 1)
                    if f:
                        hidden_high(act, l, f - 1)
                elif k == "last_split":
                    hidden_high(act, l, FT - 1)

        def hidden_high(act, l, f):
            rows = P if f < FT - 1 else FTAIL
            act.wait_ge(hidden_full.sem, hidden_full.at(l, f + 1))
            nc.scalar.copy(hid_hi[0:rows, f], hfull[0:rows, f % 2]).then_inc(hidhi_ready.sem, 1)

        with act.Fori(0, DEPTH - 1) as l:
            layer(l, False)
        layer(DEPTH - 1, True)

    @block.gpsimd
    def _(pool):
        nc.gpsimd.sem_inc(lo_ready.sem, 2)
        nc.gpsimd.sem_inc(parts_rotated.sem, 2)
        for c in range(2):
            for t in range(4):
                split_lo(pool, 0, c, t)
        pool.wait_ge(tables_loaded.sem, 48)

        def layer(l, last):
            pool.wait_ge(rotated.sem, rotated.at(l, 0))
            pool.wait_ge(tables_loaded.sem, 48)
            for j in range(4):
                ins = nc.gpsimd.tensor_tensor(cur_tab[:, j], base_tab[:, j],
                                              scales[:, j // 2, bass.ds(l, 1)].rearrange("p o d -> p (o d)"), ALU.mult)
            ins.then_inc(tabs_ready.sem, 2)
            pool.wait_ge(tabs_ready.sem, tabs_ready.at(l, 2))
            for n, s in enumerate(steps):
                k = s[0]
                if k == "normalise":
                    u = s[1]
                    r = rot_no[u]
                    j = 2 * (QKV_UNITS[u][0] % 3)
                    pool.wait_ge(rotated.sem, rotated.at(l, r - 1))
                    pool.wait_ge(normed.sem, normed.at(l, r + 1))
                    src = qn[:, r % 2].rearrange("p (h d) -> p h d", h=8)
                    for buf, jj in ((rot_buf(u), j), (turned_half[:, r % 2], j + 1)):
                        ins = nc.gpsimd.tensor_tensor(buf.rearrange("p (h d) -> p h d", h=8), src,
                                                      cur_tab[:, jj:jj + 1].to_broadcast([P, 8, DH]), ALU.mult)
                    ins.then_inc(parts_rotated.sem, 1)
                elif k == "shift":
                    b = s[1]
                    if b == 0:
                        pool.wait_ge(layer_loaded.sem, layer_loaded.at(l, 16 * LAYER_DMAS))
                    pool.wait_ge(ln_normed.sem, ln_normed.at(l, b + 1))
                    nc.gpsimd.tensor_tensor(xn[:, b % 2], xn[:, b % 2], gB[:], ALU.mult).then_inc(ln_scaled.sem, 1)
                    pool.wait_ge(ln_scaled.sem, ln_scaled.at(l, b + 1))
                    nc.gpsimd.tensor_tensor(xn[:, b % 2], xn[:, b % 2], bB[:], ALU.add).then_inc(ln_ready.sem, 1)
                elif k == "gate" and s[1] in (2, 4, 6, 8):
                    b = s[1] // 2 - 1
                    nc.gpsimd.tensor_tensor(X[:, b], X[:, b], b2B[:], ALU.add).then_inc(x_biased.sem, 1)
                for ll, c, t in splits(n, l, last):
                    split_lo(pool, ll, c, t)

        with pool.Fori(0, DEPTH - 1) as l:
            layer(l, False)
        layer(DEPTH - 1, True)

    @block.vector
    def _(dve):
        nc.vector.memset(half_log[:], float(0.5 * np.log(LN_SHIFT)))
        nc.vector.memset(kD[:], 0.0).then_inc(zero_ready.sem, 1)
        nc.vector.sem_inc(turn_read_dve.sem, 2)
        nc.vector.sem_inc(sumsq_ready.sem, 2)
        nc.vector.sem_inc(rotated.sem, 2)
        nc.vector.sem_inc(scores_read.sem, 1)
        nc.vector.sem_inc(x_new.sem, NB)

        def layer(l, last):
            for n, s in enumerate(steps):
                k = s[0]
                if k == "turn_x" or k == "turn_n":
                    b = s[1]
                    e = turn_no[(k, b, 0)]
                    j = b if k == "turn_x" else NB + b
                    dve.wait_ge(xhi_ready.sem, xhi_ready.at(l, j + 1))
                    nc.vector.tensor_tensor(xt_lo[:, :, b * P:(b + 1) * P],
                                            turnb[e % 2].rearrange("p (k t) -> p k t", k=4),
                                            xt_hi[:, :, b * P:(b + 1) * P].bitcast(F32),
                                            ALU.subtract).then_inc(turn_read_dve.sem, 1)
                elif k == "empty" and s[1] in rot_no:
                    u = s[1]
                    r = rot_no[u]
                    dve.wait_ge(squared.sem, squared.at(l, r + 1))
                    nc.vector.tensor_reduce(ss[:, r % 2], sq.rearrange("p (h d) -> p h d", h=8), AX.X,
                                            ALU.add).then_inc(sumsq_ready.sem, 1)
                    dve.wait_ge(sumsq_ready.sem, sumsq_ready.at(l, 2 * r + 1))
                    nc.vector.tensor_scalar(ss[:, r % 2], ss[:, r % 2], 1e-24, -0.5, ALU.max,
                                            ALU.mult).then_inc(sumsq_ready.sem, 1)
                elif k == "normalise":
                    u = s[1]
                    r = rot_no[u]
                    dve.wait_ge(parts_rotated.sem, parts_rotated.at(l, r - 1))
                    dve.wait_ge(rnorm_ready.sem, rnorm_ready.at(l, r + 1))
                    newton(l, rn[:, r % 2], ss[:, r % 2], r)
                    nc.vector.tensor_tensor(qn[:, r % 2].rearrange("p (h d) -> p h d", h=8),
                                            proj[u % 3].rearrange("p (h d) -> p h d", h=8),
                                            rn[:, r % 2].unsqueeze(2).to_broadcast([P, 8, DH]),
                                            ALU.mult).then_inc(normed.sem, 1)
                elif k == "rotate":
                    u = s[1]
                    r = rot_no[u]
                    dve.wait_ge(parts_rotated.sem, parts_rotated.at(l, r + 1))
                    q4 = rot_buf(u).rearrange("p (h s d) -> p h s d", h=8, s=2)
                    t4 = turned_half[:, r % 2].rearrange("p (h s d) -> p h s d", h=8, s=2)
                    nc.vector.tensor_tensor(q4[:, :, 0], q4[:, :, 0], t4[:, :, 1], ALU.add)
                    nc.vector.tensor_tensor(q4[:, :, 1], q4[:, :, 1], t4[:, :, 0], ALU.add).then_inc(rotated.sem, 1)
                elif k == "empty" and s[1] < NQ:
                    u = s[1]
                    dve.wait_ge(proj_done.sem, proj_done.at(l, u + 1))
                    nc.vector.tensor_copy(vrow[:, QKV_UNITS[u][1]], proj[u % 3][:]).then_inc(v_ready.sem, 1)
                elif k == "empty":
                    u = s[1]
                    b = WO_UNITS[u - NQ][1]
                    dve.wait_ge(proj_done.sem, proj_done.at(l, u + 1))
                    if u >= NQ + NB:
                        dve.wait_ge(x_added.sem, x_added.at(l, u - NQ - NB + 1))
                    nc.vector.tensor_tensor(X[:, b], proj[u % 3][:], X[:, b], ALU.add).then_inc(x_added.sem, 1)
                elif k == "turn_qk":
                    a = s[1]
                    e = turn_no[(k, a, 0)]
                    dve.wait_ge(turned.sem, turned.at(l, e + 1))
                    nc.vector.tensor_copy(qT[:, a % 2],
                                          turnb[0].rearrange("p (h t) -> p h t", h=4)).then_inc(turn_read_dve.sem, 1)
                elif k == "scores":
                    a = s[1]
                    dve.wait_ge(scored.sem, scored.at(l, a + 1))
                    nc.vector.tensor_tensor(prob[:, a % 2], score[:],
                                            maskadd[:, :].unsqueeze(1).to_broadcast([P, 8, P]),
                                            ALU.add).then_inc(scores_read.sem, 1)
                    dve.wait_ge(scores_read.sem, scores_read.at(l, a + 1))
                    nc.vector.tensor_reduce(rowmax[:], prob[:, a % 2], AX.X, ALU.max).then_inc(max_ready.sem, 1)
                    dve.wait_ge(max_ready.sem, max_ready.at(l, a + 1))
                    nc.vector.tensor_scalar(negmax[:, a % 2], rowmax[:], -QK_SCALE, None,
                                            ALU.mult).then_inc(negmax_ready.sem, 1)
                elif k == "values":
                    a = s[1]
                    b, hf = a % NB, a // NB
                    dve.wait_ge(probs_ready.sem, probs_ready.at(l, a + 1))
                    nc.vector.reciprocal(rsums[:], psums[:, a % 2]).then_inc(recip_ready.sem, 1)
                    dve.wait_ge(recip_ready.sem, recip_ready.at(l, a + 1))
                    nc.vector.tensor_tensor(prob[:, a % 2], prob[:, a % 2],
                                            rsums[:].unsqueeze(2).to_broadcast([P, 8, P]),
                                            ALU.mult).then_inc(probs_normed.sem, 1)
                    e = turn_no[(k, a, 1)]
                    dve.wait_ge(turned.sem, turned.at(l, e + 1))
                    nc.vector.tensor_copy(probT[:, a % 2, 4:8],
                                          turnb[1].rearrange("p (h t) -> p h t", h=4)).then_inc(turn_read_dve.sem, 1)
                    dve.wait_ge(mixhi_ready.sem, mixhi_ready.at(l, a + 1))
                    rng = mixT_hi[:, 4 * hf:4 * hf + 4, b * P:(b + 1) * P]
                    nc.vector.tensor_tensor(mixT_lo[:, 4 * hf:4 * hf + 4, b * P:(b + 1) * P],
                                            mix.rearrange("p (h t) -> p h t", h=4), rng.bitcast(F32),
                                            ALU.subtract).then_inc(mixlo_ready.sem, 1)
                elif k == "shift":
                    b = s[1]
                    dve.wait_ge(x_added.sem, x_added.at(l, NB + b + 1))
                    nc.vector.bn_stats(stats[:, 0:6], X[:, b, 0:256])
                    dve.wait_ge(mix_done.sem, mix_done.at(l, mix_no[s] + 1))
                    nc.vector.bn_stats(stats[:, 6:12], mix[:, 0:256]).then_inc(stats_ready.sem, 1)
                    dve.wait_ge(stats_ready.sem, stats_ready.at(l, 3 * b + 1))
                    nc.vector.sem_inc(stats_seen.sem, 1)
                    nc.vector.bn_aggr(meanvar[:, b % 2], stats[:]).then_inc(stats_ready.sem, 1)
                    dve.wait_ge(stats_ready.sem, stats_ready.at(l, 3 * b + 2))
                    nc.vector.tensor_scalar(halfvar[:, b % 2:b % 2 + 1], meanvar[:, b % 2, 1:2], 1e-5, -0.5, ALU.add,
                                            ALU.mult).then_inc(stats_ready.sem, 1)
                    if b >= 2:
                        dve.wait_ge(turned.sem, turned.at(l, turn_no[("turn_n", b - 2, 0)] + 1))
                    dve.wait_ge(rstd_ready.sem, rstd_ready.at(l, b + 1))
                    newton(l, rstd[:, b % 2:b % 2 + 1], halfvar[:, b % 2:b % 2 + 1], NROT + b)
                    nc.vector.tensor_scalar(xn[:, b % 2, 0:256], X[:, b, 0:256], meanvar[:, b % 2, 0:1],
                                            rstd[:, b % 2:b % 2 + 1], ALU.subtract, ALU.mult)
                    nc.vector.tensor_scalar(xn[:, b % 2, 256:512], mix[:, 0:256], meanvar[:, b % 2, 0:1],
                                            rstd[:, b % 2:b % 2 + 1], ALU.subtract, ALU.mult).then_inc(ln_normed.sem, 1)
                elif k == "value":
                    f = s[1]
                    rows = P if f < FT - 1 else FTAIL
                    u = U_W1 + 2 * f + 1
                    dve.wait_ge(gate_read.sem, gate_read.at(l, f + 1))
                    if f >= 2:
                        dve.wait_ge(hidlo_ready.sem, hidlo_ready.at(l, f - 1))
                    dve.wait_ge(proj_done.sem, proj_done.at(l, u + 1))
                    nc.vector.scalar_tensor_tensor(out=hfull[0:rows, f % 2], in0=proj[u % 3][0:rows],
                                                   scalar=b1T[0:rows, FT + f:FT + f + 1], in1=gate_out[0:rows, f % 2],
                                                   op0=ALU.add, op1=ALU.mult).then_inc(hidden_full.sem, 1)
                    if f:
                        hidden_low(l, f - 1)
                elif k == "last_split":
                    hidden_low(l, FT - 1)
                elif k == "add_down":
                    b = s[1]
                    u = U_W2 + b
                    dve.wait_ge(x_biased.sem, x_biased.at(l, b + 1))
                    dve.wait_ge(proj_done.sem, proj_done.at(l, u + 1))
                    src = proj[u % 3] if b < 3 else mix
                    nc.vector.tensor_tensor(X[:, b], src[:], X[:, b], ALU.add).then_inc(x_new.sem, 1)

        def newton(l, y, minus_half, no):
            t = step_tmp[:, 0:y.shape[1]]
            nc.vector.tensor_tensor(t, y, y, ALU.mult).then_inc(newton_step.sem, 1)
            dve.wait_ge(newton_step.sem, newton_step.at(l, 3 * no + 1))
            nc.vector.tensor_tensor(t, t, minus_half, ALU.mult).then_inc(newton_step.sem, 1)
            dve.wait_ge(newton_step.sem, newton_step.at(l, 3 * no + 2))
            nc.vector.scalar_tensor_tensor(out=y, in0=t, scalar=1.5, in1=y, op0=ALU.add,
                                           op1=ALU.mult).then_inc(newton_step.sem, 1)
            dve.wait_ge(newton_step.sem, newton_step.at(l, 3 * no + 3))

        def hidden_low(l, f):
            rows = P if f < FT - 1 else FTAIL
            dve.wait_ge(hidhi_ready.sem, hidhi_ready.at(l, f + 1))
            nc.vector.tensor_tensor(hid_lo[0:rows, f], hfull[0:rows, f % 2], hid_hi[0:rows, f].bitcast(F32),
                                    ALU.subtract).then_inc(hidlo_ready.sem, 1)

        with dve.Fori(0, DEPTH - 1) as l:
            layer(l, False)
        layer(DEPTH - 1, True)
        for b in range(NB):
            dve.wait_ge(x_new.sem, x_new.at(DEPTH - 1, b + 1))
            nc.vector.tensor_tensor(X[:, b], X[:, b], OUTER[:, b], ALU.add).then_inc(sum_ready.sem, 1)

    @block.tensor
    def _(pe):
        nc.tensor.sem_inc(down_used.sem, 3)
        nc.tensor.sem_inc(proj_done.sem, 1)

        def bank_free(l, u):
            v = u - 3
            if v < 0:
                pe.wait_ge(x_new.sem, x_new.at(l, u + 1 - NB))
            elif v in rot_no:
                pe.wait_ge(normed.sem, normed.at(l, rot_no[v] + 1))
            elif v < NQ:
                pe.wait_ge(v_ready.sem, v_ready.at(l, v_no[v] + 1))
            elif v < U_W1:
                pe.wait_ge(x_added.sem, x_added.at(l, v - NQ + 1))
            elif (v - U_W1) % 2 == 0:
                pe.wait_ge(gate_read.sem, gate_read.at(l, (v - U_W1) // 2 + 1))
            else:
                pe.wait_ge(hidden_full.sem, hidden_full.at(l, (v - U_W1) // 2 + 1))

        def turn_bank_free(l, e):
            v = e - 2
            back = v < 0
            if back:
                v += NTURN
            if v in turn_act:
                pe.wait_ge(turn_read_act.sem, turn_read_act.at(l, turn_act[v] + 1 - (len(turn_act) if back else 0)))
            else:
                pe.wait_ge(turn_read_dve.sem, turn_read_dve.at(l, turn_dve[v] + 1 - (len(turn_dve) if back else 0)))

        def three_passes(dst, lhs, rhs, first, last):
            (lh, ll), (rh, rl) = lhs, rhs
            nc.tensor.matmul(dst, lh, rh, start=first, stop=False)
            nc.tensor.matmul(dst, lh, rl, start=False, stop=False)
            return nc.tensor.matmul(dst, ll, rh, start=False, stop=last)

        def layer(l, last):
            for n, s in enumerate(steps):
                k = s[0]
                c = chunks_of(s)
                if c is not None and first_use[c] == n:
                    pe.wait_ge(lo_ready.sem, lo_ready.at(l, c + 1))
                if k == "turn_x":
                    b = s[1]
                    e = turn_no[(k, b, 0)]
                    turn_bank_free(l, e)
                    pe.wait_ge(x_new.sem, x_new.at(l, b + 1 - NB))
                    for kt in range(4):
                        dst = turnb[e % 2][:, kt * P:(kt + 1) * P]
                        src = X[:, b, kt * P:(kt + 1) * P]
                        if kt < 2:
                            ins = nc.tensor.transpose(dst, src, ident[:])
                        else:
                            ins = nc.tensor.matmul(dst, src, shiftm[:], start=True, stop=True)
                    ins.then_inc(turned.sem, 1)
                elif k == "products":
                    u = s[1]
                    cc, b = QKV_UNITS[u] if u < NQ else WO_UNITS[u - NQ]
                    if u < NB:
                        pe.wait_ge(turn_read_dve.sem, turn_read_dve.at(l, turn_dve[turn_no[("turn_x", b, 0)]] + 1))
                    if u >= NQ:
                        hf = cc - C_WO
                        pe.wait_ge(mixlo_ready.sem, mixlo_ready.at(l, hf * NB + b + 1))
                    bank_free(l, u)
                    for kt in range(4):
                        if u < NQ:
                            lhs = tuple(x[:, kt, b * P:(b + 1) * P] for x in (xt_hi, xt_lo))
                        else:
                            lhs = tuple(x[:, 4 * hf + kt, b * P:(b + 1) * P] for x in (mixT_hi, mixT_lo))
                        rhs = tuple(x[cc % 3][:, kt] for x in (whi, wlo))
                        ins = three_passes(proj[u % 3][:], lhs, rhs, kt == 0, kt == 3)
                    ins.then_inc(proj_done.sem, 1)
                elif k == "turn_qk":
                    a = s[1]
                    b, hf = a % NB, a // NB
                    need = max(rot_no[u] for u in rot_units if QKV_UNITS[u][1] == b and QKV_UNITS[u][0] // 3 == hf)
                    pe.wait_ge(rotated.sem, rotated.at(l, need + 1))
                    for g, rows in enumerate((qrow, krow)):
                        e = turn_no[(k, a, g)]
                        turn_bank_free(l, e)
                        for h in range(4):
                            ins = nc.tensor.transpose(turnb[g][:, h * P:(h + 1) * P], rows[:, b, h * P:(h + 1) * P],
                                                      ident[:])
                        ins.then_inc(turned.sem, 1)
                elif k == "scores":
                    a = s[1]
                    pe.wait_ge(zero_ready.sem, zero_ready.at(0, 1))
                    pe.wait_ge(turn_read_dve.sem, turn_read_dve.at(l, turn_dve[turn_no[("turn_qk", a, 0)]] + 1))
                    pe.wait_ge(turn_read_act.sem, turn_read_act.at(l, turn_act[turn_no[("turn_qk", a, 1)]] + 1))
                    pe.wait_ge(scores_read.sem, scores_read.at(l, a))
                    for h in range(4):
                        ins = nc.tensor.matmul(score[:, 2 * h:2 * h + 2].rearrange("p h t -> p (h t)"), qT[:, a % 2, h],
                                               kD[:, a % 2, h].rearrange("p e t -> p (e t)"), start=True, stop=True)
                    ins.then_inc(scored.sem, 1)
                elif k == "values":
                    a = s[1]
                    b = a % NB
                    pe.wait_ge(probs_normed.sem, probs_normed.at(l, a + 1))
                    for g in range(2):
                        turn_bank_free(l, turn_no[(k, a, g)])
                        for h in range(4):
                            ins = nc.tensor.transpose(turnb[g][:, h * P:(h + 1) * P], prob[:, a % 2, 4 * g + h],
                                                      ident[:])
                        ins.then_inc(turned.sem, 1)
                    uv = QKV_UNITS.index((3 * (a // NB) + 2, b))
                    pe.wait_ge(v_ready.sem, v_ready.at(l, v_no[uv] + 1))
                    if a:
                        pe.wait_ge(mixlo_ready.sem, mixlo_ready.at(l, a))
                    else:
                        pe.wait_ge(x_new.sem, x_new.at(l, 0))
                    pe.wait_ge(turn_read_act.sem, turn_read_act.at(l, turn_act[turn_no[(k, a, 0)]] + 1))
                    for h in range(8):
                        if h == 4:
                            pe.wait_ge(turn_read_dve.sem, turn_read_dve.at(l, turn_dve[turn_no[(k, a, 1)]] + 1))
                        r = 64 * (h % 2)
                        ins = nc.tensor.matmul(mix[r:r + 64, (h // 2) * P:(h // 2 + 1) * P],
                                               vrow[:, b, h * DH:(h + 1) * DH], probT[:, a % 2, h], start=True, stop=True)
                    ins.then_inc(mix_done.sem, 1)
                elif k == "shift":
                    b = s[1]
                    if b:
                        pe.wait_ge(ln_normed.sem, ln_normed.at(l, b))
                    else:
                        pe.wait_ge(mixlo_ready.sem, mixlo_ready.at(l, 2 * NB))
                    pe.wait_ge(x_added.sem, x_added.at(l, NB + b + 1))
                    nc.tensor.matmul(mix[:, 0:256], shiftm[:], X[:, b, 256:512], start=True,
                                     stop=True).then_inc(mix_done.sem, 1)
                elif k == "turn_n":
                    b = s[1]
                    e = turn_no[(k, b, 0)]
                    turn_bank_free(l, e)
                    pe.wait_ge(ln_ready.sem, ln_ready.at(l, b + 1))
                    for kt in range(4):
                        ins = nc.tensor.transpose(turnb[e % 2][:, kt * P:(kt + 1) * P],
                                                  xn[:, b % 2, kt * P:(kt + 1) * P], ident[:])
                    ins.then_inc(turned.sem, 1)
                elif k == "gate" or k == "value":
                    f = s[1]
                    g = 0 if k == "gate" else 1
                    u = U_W1 + 2 * f + g
                    rows = P if f < FT - 1 else FTAIL
                    col = 256 * g + P * (f % 2)
                    if f == 0 and g == 0:
                        pe.wait_ge(turn_read_dve.sem, turn_read_dve.at(l, turn_dve[turn_no[("turn_n", 3, 0)]] + 1))
                    bank_free(l, u)
                    for kt in range(4):
                        lhs = tuple(x[c % 3][:, kt, col:col + rows] for x in (whi, wlo))
                        ins = three_passes(proj[u % 3][0:rows], lhs, (xt_hi[:, kt], xt_lo[:, kt]), kt == 0, kt == 3)
                    ins.then_inc(proj_done.sem, 1)
                elif k == "down":
                    _, cc, b = s
                    u = U_W2 + b
                    if cc == 0:
                        if b < 3:
                            bank_free(l, u)
                        else:
                            pe.wait_ge(ln_normed.sem, ln_normed.at(l, NB))
                    dst = proj[u % 3] if b < 3 else mix
                    for t in range(npieces(c)):
                        f = 3 * cc + t
                        if b == 0:
                            pe.wait_ge(hidlo_ready.sem, hidlo_ready.at(l, f + 1))
                        rows = P if f < FT - 1 else FTAIL
                        lhs = tuple(x[0:rows, f, b * P:(b + 1) * P] for x in (hid_hi, hid_lo))
                        rhs = tuple(x[c % 3][0:rows, t] for x in (whi, wlo))
                        ins = three_passes(dst[:], lhs, rhs, f == 0, f == FT - 1)
                    if f == FT - 1:
                        ins.then_inc(proj_done.sem, 1)
                    elif b == NB - 1:
                        ins.then_inc(down_used.sem, 1)
        with pe.Fori(0, DEPTH - 1) as l:
            layer(l, False)
        layer(DEPTH - 1, True)


_X = ["Wq", "bq", "Wk", "bk", "Wv", "bv", "Wo", "bo"]
_A = ["wq", "wk_down", "wv_down", "wk_up", "wv_up", "wo"]
_F = ["Wqkv", "q_scale", "k_scale", "Wo", "ln_g", "ln_b", "W1", "b1", "W2", "b2"]
_INS = (["x", "ctx_512"] + ["L0_xattn_" + n for n in _X] + ["L0_attn_" + n for n in _A] + ["L0_ffn_" + n for n in _F])


def perceiver_block(nc, ins, out):
    with ExitStack() as ctx:
        def sb(name, shape):
            return ctx.enter_context(nc.sbuf_tensor(name, shape, F32))

        X = sb("X", [P, NB, 512])
        OUTER = sb("OUTER", [P, NB, 512])
        ident, shiftm, maskadd = sb("ident", [P, P]), sb("shiftm", [P, P]), sb("maskadd", [P, P])
        rows, cols = np.arange(P)[:, None], np.arange(P)[None]
        consts = np.stack([np.eye(P), np.eye(P, k=1), np.where(cols <= rows, 0.0, MASKED)], 1).astype(np.float32)
        consts_dram = nc.inline_tensor(consts, "square_consts").ap()
        rotary_dram = nc.inline_tensor(rotary_factors(), "rotary_factors").ap()
        consts_loaded = ctx.enter_context(nc.semaphore("consts_loaded"))
        with nc.Block() as block:
            @block.sync
            def _(sp):
                for k, tile in enumerate((ident, shiftm, maskadd)):
                    sp.dma_start(tile[:], consts_dram[:, k]).then_inc(consts_loaded, 16)
                sp.wait_ge(consts_loaded, 48)
        tabs = (ident, shiftm, maskadd, rotary_dram)
        nx, na = 2 + len(_X), 2 + len(_X) + len(_A)
        with ExitStack() as part:
            two_attentions(nc, part, tabs, X, OUTER, ins[0], ins[1], ins[2:nx], ins[nx:na])
        with ExitStack() as part:
            local_transformer(nc, part, tabs, X, OUTER, out, ins[na:])


def kernel(**inputs):
    import numpy as _np
    import concourse.bacc as _bacc
    from concourse import mybir as _mybir
    from concourse.bass_utils import run_bass_kernel_spmd as _run

    nc = _bacc.Bacc("TRN2", target_bir_lowering=False, num_devices=1)
    arrays, args = {}, []
    for name in _INS:
        a = _np.ascontiguousarray(inputs[name])
        arrays[f"in_{name}_dram"] = a
        args.append(nc.dram_tensor(f"in_{name}_dram", a.shape, _mybir.dt.from_np(a.dtype), kind="ExternalInput").ap())
    out = nc.dram_tensor("out_0_dram", inputs["x"].shape, _mybir.dt.from_np(_np.dtype("float32")),
                         kind="ExternalOutput").ap()
    perceiver_block(nc, args, out)
    r = _run(nc, [arrays], core_ids=[0])
    return r.results[0]["out_0_dram"]
```

```python
from contextlib import ExitStack

import numpy as np

import concourse.bass as bass
from concourse import mybir

P = 128
NB = 4
F32 = mybir.dt.float32
F32R = mybir.dt.float32r
ALU = mybir.AluOpType
ACT = mybir.ActivationFunctionType
AX = mybir.AxisListType
MASKED = -1e25
LN_SHIFT = 2.0 ** 20
CHUNKS_AHEAD = (("qkv", 0, 0), ("qkv", 1, 0))
LN_EXP_SET = "natural_log_exp_and_others"


class Signal:

    def __init__(self, sem, per, first=0):
        self.sem, self.per, self.first = sem, per, first

    def at(self, turn, n):
        return turn * self.per + (self.first + n)


def rotary_factors():
    half = np.arange(0, 64, 2, dtype=np.float32)
    inv_freq = (1.0 / 10000.0 ** (half / 64)).astype(np.float32)
    t = np.arange(P, dtype=np.float32)
    freqs = t[:, None] * inv_freq[None, :]
    base = (half + np.float32(0.4 * 64)) / np.float32(1.4 * 64)
    scale = base[None, :] ** ((t - P // 2) / np.float32(64))[:, None]
    cos, sin = np.cos(freqs), np.sin(freqs)
    tabs = []
    for s in (8.0 * scale, 1.0 / scale):
        tabs += [np.concatenate([cos * s, cos * s], -1), np.concatenate([sin * s, -sin * s], -1)]
    return np.stack(tabs, 1).astype(np.float32)


def two_attentions(nc, ctx, tabs, X, OUTER, shared, ahead, x_dram, ctx_dram, xw, aw):
    Wq, bq, Wk, bk, Wv, bv, Wo, bo = xw
    wq, wk_down, wv_down, wk_up, wv_up, wo = aw
    S, DC = ctx_dram.shape[1:]
    D = x_dram.shape[2]
    H, DK = 16, 32
    HA, GA, DH, DL = 8, 2, 128, 32
    NC = S // 512
    KT = D // P
    SCALE, SCALE_A = float(DK) ** -0.5, float(DH) ** -0.5

    ident, shiftm, maskadd, _ = tabs

    def sb(name, shape, dt=F32):
        return ctx.enter_context(nc.sbuf_tensor(name, shape, dt))

    def ps(name, shape):
        return ctx.enter_context(nc.psum_tensor(name, shape, F32))

    def signal(name, per, first=0):
        return Signal(ctx.enter_context(nc.semaphore(name)), per, first)

    ahead_hi, ahead_lo, ahead_raw = shared
    wkv_hi, wkv_lo = (t[0].rearrange("p (t n) -> p t n", t=2) for t in (ahead_hi, ahead_lo))
    cT_hi, cT_lo = (t[1].rearrange("p (s t n) -> p s t n", s=2, t=2) for t in (ahead_hi, ahead_lo))
    cin = ahead_raw[0].rearrange("p (s t n) -> p s t n", s=2, t=4)
    Wq_sb = ahead_raw[1].rearrange("p (t n) -> p t n", t=KT)
    Wo_sb = sb("Wo_sb", [P, KT, D])
    wq_sb = sb("wq_sb", [P, KT, HA * DH])
    down = sb("down", [P, KT, 2, GA * DL])
    up = sb("up", [DL, 2, DH])
    bqT = sb("bqT", [P, KT])
    bkT = sb("bkT", [P, KT])
    bvB = sb("bvB", [P, D])
    boB = sb("boB", [P, D])
    xin = sb("xin", [P, D])
    xbo = sb("xbo", [P, D])
    xn = sb("xn_a", [P, D])
    xnT = sb("xnT", [P, KT, P])
    xq = sb("xq", [P, D])
    xqT = sb("xqT", [P, KT, P])
    x1 = sb("x1", [P, D])
    kT = sb("kT", [P, KT, S])
    vrow = sb("vrow_a", [P, S // P, D])
    wo_sb = vrow[:, S // P - HA:]
    qpad = sb("qpad", [P, H, P])
    prob = sb("prob_a", [P, 2, S])
    probT = sb("probT_a", [P, 3, 512])
    mixT = xnT
    recB, recT = xn, xnT.rearrange("p k t -> p (k t)")
    qT_a = prob[:, 0, 0:1024].rearrange("p (h t) -> p h t", h=HA)
    mixT_b = prob[:, 0, 1024:2048].rearrange("p (h t) -> p h t", h=HA)
    prob_b = prob[:, 1, 0:1024].rearrange("p (h t) -> p h t", h=HA)
    probT_b = prob[:, 1, 1024:2048].rearrange("p (h t) -> p h t", h=HA)
    lat = sb("lat", [DL, 4, P])
    kv_a = probT[:, 2].rearrange("p (i t) -> p i t", i=4)
    SPANS = ((0, 1), (1, 2), (2, 4))
    rmax4 = sb("rmax4", [P, 4])
    rmax = sb("rmax", [P, 8])
    nmax = sb("nmax", [P, 8])
    sums = sb("sums", [P, len(SPANS), H])
    total = sb("total", [P, H])
    rsum = sb("rsum", [P, H])
    stats = sb("stats_a", [P, 6])
    meanvar = sb("meanvar_a", [P, 2])
    halfvar = sb("halfvar_a", [P, 1])
    lnbuf = sb("lnbuf_a", [P, 1])
    rstd = sb("rstd_a", [P, 1])
    step_tmp = sb("step_tmp_a", [P, 1])

    score = ps("score_a", [P, 4, 512])
    turnb = ps("turn_a", [P, 2, 512])
    outb = ps("out_a", [P, 512])
    miscb = ps("misc_a", [P, 512])

    weights_loaded = signal("weights_loaded", 0)
    wo_loaded = signal("wo_loaded", 16)
    kv_loaded = signal("kv_loaded", 0)
    bias_loaded = signal("bias_loaded", 0)
    wq_loaded = signal("wq_loaded", 0)
    wkv_hi_ready = signal("wkv_hi_ready", 0)
    wkv_ready = signal("wkv_ready", 0)
    cleared = signal("cleared", 0)
    x_loaded = signal("x_loaded", 16)
    c_loaded = [signal(f"c_loaded{i}", 16 * NC // 2) for i in range(2)]
    NORMS = ("rows", "middle", "last")
    stats_ready = [signal(f"stats_ready_{n}", 3) for n in NORMS]
    stats_seen = signal("stats_seen_a", 3)
    logs_ready = [signal(f"logs_ready_{n}", 1) for n in NORMS]
    rstd_ready = [signal(f"rstd_ready_{n}", 1) for n in NORMS]
    newton_step = [signal(f"newton_step_{n}", 3) for n in NORMS]
    xq_ready = signal("xq_ready", 1)
    xn_ready = signal("xn_ready_a", 1)
    xqT_done = signal("xqT_done", 1)
    xqT_ready = signal("xqT_ready", 1)
    xnT_done = signal("xnT_done", 1)
    xnT_ready = signal("xnT_ready", 1)
    q_done = signal("q_done", 1)
    q_ready = signal("q_ready", 1)
    cT_done = signal("cT_done", NC, 1)
    chi_ready = signal("chi_ready", NC)
    clo_ready = signal("clo_ready", NC)
    kv_done = signal("kv_done", 8 * NC)
    k_ready = signal("k_ready", 4 * NC)
    v_ready = signal("v_ready_a", 4 * NC)
    s_done = signal("s_done", 4 * H)
    chunkmax_ready = signal("chunkmax_ready", 4 * H)
    max_ready = signal("max_ready_a", H)
    nmax_ready = signal("nmax_ready", H)
    p_ready = signal("p_ready", len(SPANS) * H)
    pT_done = signal("pT_done", 4 * H)
    pT_act = signal("pT_act", H)
    pT_dve = signal("pT_dve", 3 * H)
    pv_done = signal("pv_done", H)
    rec_ready = signal("rec_ready", 3)
    recT_done = signal("recT_done", 1)
    recT_ready = signal("recT_ready", 1)
    mixT_ready = signal("mixT_ready_a", 1)
    y_done = signal("y_done", 2)
    xbo_ready = signal("xbo_ready", 1)
    x1_ready = signal("x1_ready", 1, 1)
    x2_ready = signal("x2_ready", 1, 1)
    lat_done = signal("lat_done", 2)
    qa_ready = signal("qa_ready", 1)
    lat_ready = signal("lat_ready", 1)
    kva_done = signal("kva_done", 1)
    kva_ready = signal("kva_ready", 1)
    sb_done = signal("scores_b_done", 1)
    masked = signal("masked_b", 3)
    pb_ready = signal("probs_b_ready", 1)
    pb_normed = signal("probs_b_normed", 2)
    pTb_done = signal("pTb_done", 2)
    pTb_act = signal("pTb_act", 1)
    pTb_dve = signal("pTb_dve", 1)
    ob_done = signal("ob_done", 2)
    ob_act = signal("ob_act", 1)
    ob_dve = signal("ob_dve", 1)
    x_out = signal("x_out", 1, 1)
    ahead_loaded = signal("ahead_loaded", 0)
    ahead_hi_ready = signal("ahead_hi_ready", 0)
    ahead_lo_ready = signal("ahead_lo_ready", 0)

    UNITS = [(kind, i, score[:, (2 * i + (kind == "v")) % 4]) for i in range(4) for kind in ("k", "v")]
    LAST_UNITS = [("k", 0, score[:, 0]), ("v", 0, score[:, 1]), ("k", 1, score[:, 2]), ("k", 2, score[:, 3]),
                  ("k", 3, score[:, 0]), ("v", 2, turnb[:, 0]), ("v", 1, miscb[:]), ("v", 3, turnb[:, 1])]
    LAST_BANK_USER = [-4, -3, -2, -1, 0, None, None, None]

    turn_banks = [turnb[:, 0], turnb[:, 1], miscb[:], turnb[:, 0]]

    def units_of(c):
        return LAST_UNITS if c == NC - 1 else UNITS

    def kept(c, n):
        if n < 0:
            c, n = c - 1, n + 8
        kind = units_of(c)[n][0]
        return kind, 4 * c + sum(u[0] == kind for u in units_of(c)[:n + 1])

    block = ctx.enter_context(nc.Block())

    @block.sync
    def _(sp):
        raw = prob[:, 0].rearrange("p (t n) -> p t n", t=2)
        sem = weights_loaded.sem

        def load_context(b, c):
            src = ctx_dram[bass.ds(b, 1)].rearrange("o (c t p) d -> p (o c) t d", p=P, t=4)
            sp.dma_start(cin[:, c % 2], src[:, c]).then_inc(c_loaded[c % 2].sem, 16)

        load_context(0, 0)
        sp.dma_start(raw[:, :, 0:D], Wk.rearrange("(t p) n -> p t n", p=P)).then_inc(kv_loaded.sem, 16)
        sp.dma_start(raw[:, :, D:2 * D], Wv.rearrange("(t p) n -> p t n", p=P)).then_inc(kv_loaded.sem, 16)
        load_context(0, 1)
        sp.dma_start(boB[:], bo.rearrange("(o n) -> o n", o=1).to_broadcast([P, D])).then_inc(sem, 16)
        sp.dma_start(Wo_sb[:], Wo.rearrange("(t p) n -> p t n", p=P)).then_inc(sem, 16)
        sp.dma_start(wq_sb[:], wq.rearrange("(t p) n -> p t n", p=P)).then_inc(sem, 16)
        for i, w in enumerate((wk_down, wv_down)):
            sp.dma_start(down[:, :, i], w.rearrange("(t p) n -> p t n", p=P)).then_inc(sem, 16)
        for i, w in enumerate((wk_up, wv_up)):
            sp.dma_start(up[:, i], w).then_inc(sem, 16)

        def batch(b, last):
            for c in range(2, NC):
                sp.wait_ge(cT_done.sem, cT_done.at(b, c - 1))
                load_context(b, c)
            if not last:
                sp.wait_ge(xbo_ready.sem, xbo_ready.at(b, 1))
                sp.wait_ge(xq_ready.sem, xq_ready.at(b, 1))
                sp.dma_start(xin[:], x_dram[bass.ds(b + 1, 1)].rearrange("o t d -> t (o d)")).then_inc(x_loaded.sem, 16)
                for c in range(2):
                    sp.wait_ge(cT_done.sem, cT_done.at(b, NC - 1 + c))
                    load_context(b + 1, c)
            if last:
                sp.wait_ge(kv_done.sem, kv_done.at(b, 8 * NC))
                for raw, src in zip(ahead_raw, ahead):
                    sp.dma_start(raw.rearrange("p (t n) -> p t n", t=KT), src).then_inc(ahead_loaded.sem, 16)
            sp.wait_ge(pv_done.sem, pv_done.at(b, H))
            sp.dma_start(wo_sb, wo.rearrange("(t p) n -> p t n", p=P)).then_inc(wo_loaded.sem, 16)

        with sp.Fori(0, NB - 1) as b:
            batch(b, False)
        batch(NB - 1, True)

    WEIGHTS = 16 * 7

    @block.gpsimd
    def _(pool):
        pool.wait_ge(weights_loaded.sem, WEIGHTS)
        with pool.Fori(0, NB) as b:
            pool.wait_ge(x1_ready.sem, x1_ready.at(b, 0))
            pool.wait_ge(x_loaded.sem, x_loaded.at(b, 16))
            nc.gpsimd.tensor_tensor(xbo[:], xin[:], boB[:], ALU.add).then_inc(xbo_ready.sem, 1)
        for i in range(2):
            pool.wait_ge(ahead_hi_ready.sem, i + 1)
            nc.gpsimd.tensor_tensor(ahead_lo[i][:], ahead_raw[i][:], ahead_hi[i][:], ALU.subtract
                                    ).then_inc(ahead_lo_ready.sem, 1)
        pool.wait_ge(ahead_lo_ready.sem, 2)

    @block.scalar
    def _(act):
        act.dma_start(bkT[:], bk.rearrange("(g p) -> p g", p=P), allow_slow_non_contiguous=True
                     ).then_inc(bias_loaded.sem, 16)
        act.dma_start(bvB[:], bv.rearrange("(o n) -> o n", o=1).to_broadcast([P, D])).then_inc(bias_loaded.sem, 16)
        act.dma_start(xin[:], x_dram[0]).then_inc(x_loaded.sem, 16)
        act.dma_start(Wq_sb, Wq.rearrange("(t p) n -> p t n", p=P)).then_inc(wq_loaded.sem, 16)
        act.dma_start(bqT[:], bq.rearrange("(g p) -> p g", p=P), allow_slow_non_contiguous=True
                     ).then_inc(wq_loaded.sem, 16)
        nc.scalar.preload_act_table_set(LN_EXP_SET)

        def inverse_deviation(b, no):
            act.wait_ge(stats_ready[no].sem, stats_ready[no].at(b, 3))
            nc.scalar.activation(lnbuf[:], halfvar[:], ACT.Ln, scale=-2.0).then_inc(logs_ready[no].sem, 1)
            act.wait_ge(logs_ready[no].sem, logs_ready[no].at(b, 1))
            nc.scalar.activation(rstd[:], lnbuf[:], ACT.Exp, scale=-0.5).then_inc(rstd_ready[no].sem, 1)

        def turned_queries(b):
            act.wait_ge(xqT_done.sem, xqT_done.at(b, 1))
            nc.scalar.copy(xqT[:], outb.rearrange("p (k t) -> p k t", k=KT)).then_inc(xqT_ready.sem, 1)

        def context_high(b, c):
            act.wait_ge(cT_done.sem, cT_done.at(b, c + 1))
            nc.scalar.copy(cT_hi[:, c % 2], turnb[:]).then_inc(chi_ready.sem, 1)

        def keep_keys(b, c):
            for n, (kind, g, bank) in enumerate(units_of(c)):
                if kind == "k":
                    act.wait_ge(kv_done.sem, kv_done.at(b, 8 * c + n + 1))
                    nc.scalar.activation(kT[:, g, 512 * c:512 * c + 512], bank, ACT.Identity,
                                         bias=bkT[:, g:g + 1]).then_inc(k_ready.sem, 1)

        context_high(0, 0)
        act.wait_ge(kv_loaded.sem, 32)
        nc.scalar.copy(wkv_hi, prob[:, 0].rearrange("p (t n) -> p t n", t=2)).then_inc(wkv_hi_ready.sem, 1)
        context_high(0, 1)
        act.wait_ge(bias_loaded.sem, 32)
        inverse_deviation(0, 0)
        keep_keys(0, 0)
        turned_queries(0)

        def batch(b, last):
            for c in range(1, NC):
                if c + 1 < NC:
                    context_high(b, c + 1)
                keep_keys(b, c)
            for h in range(H + 1):
                if h:
                    act.wait_ge(pT_done.sem, pT_done.at(b, 4 * h - 3))
                    nc.scalar.copy(probT[:, 0], turn_banks[0]).then_inc(pT_act.sem, 1)
                if h < H:
                    act.wait_ge(nmax_ready.sem, nmax_ready.at(b, h + 1))
                    for g, (c0, c1) in enumerate(SPANS):
                        nc.scalar.activation(prob[:, h % 2, 512 * c0:512 * c1],
                                             score[:, c0:c1].rearrange("p c n -> p (c n)"), ACT.Exp,
                                             bias=nmax[:, 0:1], scale=SCALE,
                                             accum_out=sums[:, g, h:h + 1]).then_inc(p_ready.sem, 1)
                if h == 4 and not last:
                    inverse_deviation(b + 1, 0)
                if last and h in (6, 9):
                    act.wait_ge(ahead_loaded.sem, 32)
                    i = (h - 6) // 3
                    nc.scalar.copy(ahead_hi[i][:], ahead_raw[i][:]).then_inc(ahead_hi_ready.sem, 1)
            act.wait_ge(recT_done.sem, recT_done.at(b, 1))
            nc.scalar.copy(recT, miscb[:]).then_inc(recT_ready.sem, 1)
            if not last:
                context_high(b + 1, 0)
                turned_queries(b + 1)

            inverse_deviation(b, 1)
            act.wait_ge(xnT_done.sem, xnT_done.at(b, 1))
            nc.scalar.copy(xnT[:], miscb.rearrange("p (k t) -> p k t", k=KT)).then_inc(xnT_ready.sem, 1)
            act.wait_ge(lat_done.sem, lat_done.at(b, 1))
            nc.scalar.copy(qT_a.rearrange("p h t -> p (h t)"),
                           score[:, 0:2].rearrange("p c n -> p (c n)")).then_inc(qa_ready.sem, 1)
            if not last:
                context_high(b + 1, 1)
            act.wait_ge(masked.sem, masked.at(b, 3))
            for h in range(HA):
                ins = nc.scalar.activation(prob_b[:, h], prob_b[:, h], ACT.Exp, bias=nmax[:, h:h + 1], scale=SCALE_A,
                                           accum_out=total[:, h:h + 1])
            ins.then_inc(pb_ready.sem, 1)
            if not last:
                keep_keys(b + 1, 0)
            act.wait_ge(pTb_done.sem, pTb_done.at(b, 1))
            nc.scalar.copy(probT_b[:, 0:4].rearrange("p h t -> p (h t)"), turnb[:, 0]).then_inc(pTb_act.sem, 1)
            act.wait_ge(ob_done.sem, ob_done.at(b, 1))
            nc.scalar.copy(mixT_b[:, 0:4].rearrange("p h t -> p (h t)"), score[:, 2]).then_inc(ob_act.sem, 1)
            inverse_deviation(b, 2)

        with act.Fori(0, NB - 1) as b:
            batch(b, False)
        batch(NB - 1, True)

    @block.vector
    def _(dve):
        nc.vector.memset(qpad[:], 0.0).then_inc(cleared.sem, 1)
        nc.vector.sem_inc(x1_ready.sem, 1)
        nc.vector.sem_inc(x2_ready.sem, 1)
        nc.vector.sem_inc(x_out.sem, 1)
        dve.wait_ge(cleared.sem, 1)

        def norm(b, no, rows, out, done):
            have, steps = stats_ready[no], newton_step[no]
            nc.vector.bn_stats(stats[:], rows).then_inc(have.sem, 1)
            dve.wait_ge(have.sem, have.at(b, 1))
            nc.vector.sem_inc(stats_seen.sem, 1)
            nc.vector.bn_aggr(meanvar[:], stats[:]).then_inc(have.sem, 1)
            dve.wait_ge(have.sem, have.at(b, 2))
            nc.vector.tensor_scalar(halfvar[:], meanvar[:, 1:2], 1e-5, -0.5, ALU.add,
                                    ALU.mult).then_inc(have.sem, 1)
            dve.wait_ge(rstd_ready[no].sem, rstd_ready[no].at(b, 1))
            nc.vector.tensor_tensor(step_tmp[:], rstd[:], rstd[:], ALU.mult).then_inc(steps.sem, 1)
            dve.wait_ge(steps.sem, steps.at(b, 1))
            nc.vector.tensor_tensor(step_tmp[:], step_tmp[:], halfvar[:], ALU.mult).then_inc(steps.sem, 1)
            dve.wait_ge(steps.sem, steps.at(b, 2))
            nc.vector.scalar_tensor_tensor(out=rstd[:], in0=step_tmp[:], scalar=1.5, in1=rstd[:], op0=ALU.add,
                                           op1=ALU.mult).then_inc(steps.sem, 1)
            dve.wait_ge(steps.sem, steps.at(b, 3))
            nc.vector.tensor_scalar(out, rows, meanvar[:, 0:1], rstd[:, 0:1], ALU.subtract,
                                    ALU.mult).then_inc(done.sem, 1)

        def query_rows(b):
            dve.wait_ge(x_loaded.sem, x_loaded.at(b, 16))
            norm(b, 0, xin[:], xq[:], xq_ready)

        def spread_queries(b):
            dve.wait_ge(q_done.sem, q_done.at(b, 1))
            for j in range(4):
                r = slice(32 * j, 32 * j + 32)
                ins = nc.vector.tensor_tensor(qpad[r].rearrange("p (g j) t -> p j g t", j=4)[:, j],
                                              outb[r].rearrange("p (g t) -> p g t", g=4),
                                              bqT[r].unsqueeze(2).to_broadcast([32, 4, P]), ALU.add)
            ins.then_inc(q_ready.sem, 1)

        def context_low(b, c):
            dve.wait_ge(chi_ready.sem, chi_ready.at(b, c + 1))
            nc.vector.tensor_tensor(cT_lo[:, c % 2], turnb[:], cT_hi[:, c % 2], ALU.subtract
                                    ).then_inc(clo_ready.sem, 1)

        def keep_values(b, c, ts):
            for n, (kind, t, bank) in enumerate(units_of(c)):
                if kind == "v" and t in ts:
                    dve.wait_ge(kv_done.sem, kv_done.at(b, 8 * c + n + 1))
                    nc.vector.tensor_tensor(vrow[:, 4 * c + t], bank, bvB[:], ALU.add).then_inc(v_ready.sem, 1)

        context_low(0, 0)
        dve.wait_ge(wkv_hi_ready.sem, 1)
        nc.vector.tensor_tensor(wkv_lo, prob[:, 0].rearrange("p (t n) -> p t n", t=2), wkv_hi.bitcast(F32),
                                ALU.subtract).then_inc(wkv_ready.sem, 1)
        context_low(0, 1)
        dve.wait_ge(bias_loaded.sem, 32)
        query_rows(0)
        keep_values(0, 0, range(4))
        dve.wait_ge(wq_loaded.sem, 32)
        spread_queries(0)

        def batch(b, last):
            for c in range(1, NC):
                if c + 1 < NC:
                    context_low(b, c + 1)
                keep_values(b, c, range(4) if c + 1 < NC else (0, 2))
            for h in range(H + 1):
                if h < H:
                    for c in range(4):
                        dve.wait_ge(s_done.sem, s_done.at(b, 4 * h + c + 1))
                        nc.vector.tensor_reduce(rmax4[:, c:c + 1], score[:, c], AX.X,
                                                ALU.max).then_inc(chunkmax_ready.sem, 1)
                    dve.wait_ge(chunkmax_ready.sem, chunkmax_ready.at(b, 4 * h + 4))
                    nc.vector.tensor_reduce(rmax[:, 0:1], rmax4[:], AX.X, ALU.max).then_inc(max_ready.sem, 1)
                    dve.wait_ge(max_ready.sem, max_ready.at(b, h + 1))
                    nc.vector.tensor_scalar(nmax[:, 0:1], rmax[:, 0:1], -SCALE, None,
                                            ALU.mult).then_inc(nmax_ready.sem, 1)
                if h == 0:
                    keep_values(b, NC - 1, (1, 3))
                if h:
                    for c in (1, 2, 3):
                        dve.wait_ge(pT_done.sem, pT_done.at(b, 4 * (h - 1) + c + 1))
                        nc.vector.tensor_copy(probT[:, c % 3], turn_banks[c]).then_inc(pT_dve.sem, 1)
                if h == 4 and not last:
                    query_rows(b + 1)
            dve.wait_ge(p_ready.sem, p_ready.at(b, len(SPANS) * H))
            nc.vector.tensor_reduce(total[:], sums.rearrange("p g h -> p h g"), AX.X, ALU.add).then_inc(rec_ready.sem, 1)
            dve.wait_ge(rec_ready.sem, rec_ready.at(b, 1))
            nc.vector.reciprocal(rsum[:], total[:]).then_inc(rec_ready.sem, 1)
            dve.wait_ge(rec_ready.sem, rec_ready.at(b, 2))
            nc.vector.tensor_copy(recB.rearrange("p (h d) -> p h d", h=H),
                                  rsum[:].unsqueeze(2).to_broadcast([P, H, DK])).then_inc(rec_ready.sem, 1)
            dve.wait_ge(recT_ready.sem, recT_ready.at(b, 1))
            dve.wait_ge(pv_done.sem, pv_done.at(b, H))
            nc.vector.tensor_tensor(mixT.rearrange("p g t -> p (g t)"), outb[:], recT,
                                    ALU.mult).then_inc(mixT_ready.sem, 1)
            if not last:
                context_low(b + 1, 0)
            dve.wait_ge(xbo_ready.sem, xbo_ready.at(b, 1))
            dve.wait_ge(y_done.sem, y_done.at(b, 1))
            nc.vector.tensor_tensor(x1[:], miscb[:], xbo[:], ALU.add).then_inc(x1_ready.sem, 1)

            dve.wait_ge(x1_ready.sem, x1_ready.at(b, 1))
            norm(b, 1, x1[:], xn[:], xn_ready)
            if not last:
                spread_queries(b + 1)
            dve.wait_ge(lat_done.sem, lat_done.at(b, 2))
            nc.vector.tensor_copy(lat.rearrange("p i t -> p (i t)"), score[0:DL, 2]).then_inc(lat_ready.sem, 1)
            dve.wait_ge(kva_done.sem, kva_done.at(b, 1))
            nc.vector.tensor_copy(probT[:, 2], score[:, 3]).then_inc(kva_ready.sem, 1)
            dve.wait_ge(sb_done.sem, sb_done.at(b, 1))
            nc.vector.tensor_tensor(prob_b, score[:, 0:2].rearrange("p c (h t) -> p (c h) t", t=P),
                                    maskadd[:].unsqueeze(1).to_broadcast([P, HA, P]), ALU.add).then_inc(masked.sem, 1)
            dve.wait_ge(masked.sem, masked.at(b, 1))
            nc.vector.tensor_reduce(rmax[:], prob_b, AX.X, ALU.max).then_inc(masked.sem, 1)
            dve.wait_ge(masked.sem, masked.at(b, 2))
            nc.vector.tensor_scalar(nmax[:], rmax[:], -SCALE_A, None, ALU.mult).then_inc(masked.sem, 1)
            if not last:
                context_low(b + 1, 1)
                keep_values(b + 1, 0, (0, 1))
            dve.wait_ge(pb_ready.sem, pb_ready.at(b, 1))
            nc.vector.reciprocal(rsum[:, 0:HA], total[:, 0:HA]).then_inc(pb_normed.sem, 1)
            dve.wait_ge(pb_normed.sem, pb_normed.at(b, 1))
            nc.vector.tensor_tensor(prob_b, prob_b, rsum[:, 0:HA].unsqueeze(2).to_broadcast([P, HA, P]),
                                    ALU.mult).then_inc(pb_normed.sem, 1)
            if not last:
                keep_values(b + 1, 0, (2, 3))
            dve.wait_ge(pTb_done.sem, pTb_done.at(b, 2))
            nc.vector.tensor_copy(probT_b[:, 4:8].rearrange("p h t -> p (h t)"), turnb[:, 1]).then_inc(pTb_dve.sem, 1)
            dve.wait_ge(ob_done.sem, ob_done.at(b, 2))
            nc.vector.tensor_copy(mixT_b[:, 4:8].rearrange("p h t -> p (h t)"), score[:, 3]).then_inc(ob_dve.sem, 1)
            dve.wait_ge(y_done.sem, y_done.at(b, 2))
            out_rows, out_normed = (t[:, b] if last else t[:, bass.ds(b, 1)].rearrange("p o d -> p (o d)")
                                    for t in (OUTER, X))
            nc.vector.tensor_tensor(out_rows, miscb[:], x1[:], ALU.add)
            nc.vector.tensor_tensor(x1[:], miscb[:], x1[:], ALU.add).then_inc(x2_ready.sem, 1)
            dve.wait_ge(x2_ready.sem, x2_ready.at(b, 1))
            norm(b, 2, x1[:], out_normed, x_out)
            dve.wait_ge(x_out.sem, x_out.at(b, 1))

        with dve.Fori(0, NB - 1) as b:
            batch(b, False)
        batch(NB - 1, True)

    @block.tensor
    def _(pe):
        nc.tensor.sem_inc(cT_done.sem, 1)

        def three_passes(dst, lhs, rhs, first, last):
            (lh, ll), (rh, rl) = lhs, rhs
            nc.tensor.matmul(dst, lh, rh, start=first, stop=False)
            nc.tensor.matmul(dst, lh, rl, start=False, stop=False)
            return nc.tensor.matmul(dst, ll, rh, start=False, stop=last)

        def turn_rows(dst, rows, done):
            for k in range(KT):
                ins = nc.tensor.transpose(dst[:, k * P:(k + 1) * P], rows[:, k * P:(k + 1) * P], ident[:])
            ins.then_inc(done.sem, 1)

        def queries(b):
            pe.wait_ge(xq_ready.sem, xq_ready.at(b, 1))
            turn_rows(outb, xq, xqT_done)
            pe.wait_ge(xqT_ready.sem, xqT_ready.at(b, 1))
            for g in range(4):
                for k in range(KT):
                    ins = nc.tensor.matmul(outb[:, g * P:(g + 1) * P], Wq_sb[:, k, g * P:(g + 1) * P], xqT[:, k],
                                           start=(k == 0), stop=(k == KT - 1))
            ins.then_inc(q_done.sem, 1)

        def turn_context(b, c):
            pe.wait_ge(c_loaded[c % 2].sem, c_loaded[c % 2].at(b, 16 * (c // 2 + 1)))
            for k in range(2):
                for t in range(4):
                    ins = nc.tensor.transpose(turnb[:, k, t * P:(t + 1) * P], cin[:, c % 2, t, k * P:(k + 1) * P],
                                              ident[:])
            ins.then_inc(cT_done.sem, 1)

        def keys_and_values(b, c, ns=range(8)):
            pe.wait_ge(clo_ready.sem, clo_ready.at(b, c + 1))
            parts = (cT_hi[:, c % 2], cT_lo[:, c % 2])
            for n in ns:
                kind, i, bank = units_of(c)[n]
                before = n - 4 if c < NC - 1 else LAST_BANK_USER[n]
                if before is not None and (c or before >= 0):
                    what, count = kept(c, before)
                    done = k_ready if what == "k" else v_ready
                    pe.wait_ge(done.sem, done.at(b, count))
                for k in range(2):
                    if kind == "k":
                        lhs = tuple(w[:, k, i * P:(i + 1) * P] for w in (wkv_hi, wkv_lo))
                        rhs = tuple(x[:, k] for x in parts)
                    else:
                        lhs = tuple(x[:, k, i * P:(i + 1) * P] for x in parts)
                        rhs = tuple(w[:, k, D:2 * D] for w in (wkv_hi, wkv_lo))
                    ins = three_passes(bank, lhs, rhs, k == 0, k == 1)
                ins.then_inc(kv_done.sem, 1)

        turn_context(0, 0)
        pe.wait_ge(clo_ready.sem, 1)
        turn_context(0, 1)
        pe.wait_ge(wkv_ready.sem, 1)
        keys_and_values(0, 0)
        pe.wait_ge(wq_loaded.sem, 32)
        queries(0)
        pe.wait_ge(weights_loaded.sem, WEIGHTS)
        pe.wait_ge(cleared.sem, 1)

        def batch(b, last):
            for c in range(1, NC):
                pe.wait_ge(clo_ready.sem, clo_ready.at(b, c + 1))
                if c + 1 < NC:
                    turn_context(b, c + 1)
                if c + 1 < NC:
                    keys_and_values(b, c)
            keys_and_values(b, NC - 1, range(6))
            pe.wait_ge(q_ready.sem, q_ready.at(b, 1))
            pe.wait_ge(k_ready.sem, k_ready.at(b, 4 * NC))
            pe.wait_ge(v_ready.sem, v_ready.at(b, 4 * NC - 3))

            def turn_probs(h, c):
                if c == 3:
                    pe.wait_ge(pT_act.sem, pT_act.at(b, h + 1))
                elif h:
                    pe.wait_ge(pT_dve.sem, pT_dve.at(b, 3 * (h - 1) + (3, 1, 2)[c]))
                for t in range(4):
                    at = (4 * c + t) * P
                    ins = nc.tensor.transpose(turn_banks[c][:, t * P:(t + 1) * P], prob[:, h % 2, at:at + P], ident[:])
                ins.then_inc(pT_done.sem, 1)

            def weigh(h, c):
                r = 32 * (h % 4)
                if c == 0:
                    pe.wait_ge(pT_act.sem, pT_act.at(b, h + 1))
                else:
                    pe.wait_ge(pT_dve.sem, pT_dve.at(b, 3 * h + c))
                for t in range(4):
                    n = 4 * c + t
                    ins = nc.tensor.matmul(outb[r:r + 32, (h // 4) * P:(h // 4 + 1) * P],
                                           vrow[:, n, h * DK:(h + 1) * DK], probT[:, c % 3, t * P:(t + 1) * P],
                                           start=(n == 0), stop=(n == S // P - 1))
                if c == 3:
                    ins.then_inc(pv_done.sem, 1)

            for h in range(H + 1):
                if h == 1:
                    pe.wait_ge(x2_ready.sem, x2_ready.at(b, 0))
                    keys_and_values(b, NC - 1, range(6, 8))
                if h == H:
                    pe.wait_ge(p_ready.sem, p_ready.at(b, len(SPANS) * H))
                for c in range(4):
                    if h < H:
                        if h and c in (0, 1, 2):
                            pe.wait_ge(p_ready.sem, p_ready.at(b, len(SPANS) * (h - 1) + c + 1))
                        nc.tensor.matmul(score[:, c], qpad[:, h], kT[:, h // 4, 512 * c:512 * c + 512], start=True,
                                         stop=True).then_inc(s_done.sem, 1)
                    if c == 0 and h >= 2:
                        weigh(h - 2, 2)
                        weigh(h - 2, 3)
                if h == 1:
                    pe.wait_ge(v_ready.sem, v_ready.at(b, 4 * NC))
                if h:
                    turn_probs(h - 1, 0)
                    turn_probs(h - 1, 1)
                    turn_probs(h - 1, 2)
                    weigh(h - 1, 0)
                    turn_probs(h - 1, 3)
                    weigh(h - 1, 1)
            weigh(H - 1, 2)
            weigh(H - 1, 3)
            pe.wait_ge(rec_ready.sem, rec_ready.at(b, 3))
            pe.wait_ge(x2_ready.sem, x2_ready.at(b, 0))
            for g in range(4):
                ins = nc.tensor.transpose(miscb[:, g * P:(g + 1) * P], recB[:, g * P:(g + 1) * P], ident[:])
            ins.then_inc(recT_done.sem, 1)
            if not last:
                turn_context(b + 1, 0)
            pe.wait_ge(mixT_ready.sem, mixT_ready.at(b, 1))
            for g in range(KT):
                ins = nc.tensor.matmul(miscb[:], mixT[:, g], Wo_sb[:, g], start=(g == 0), stop=(g == KT - 1))
            ins.then_inc(y_done.sem, 1)
            if not last:
                queries(b + 1)

            pe.wait_ge(xn_ready.sem, xn_ready.at(b, 1))
            turn_rows(miscb, xn, xnT_done)
            pe.wait_ge(xnT_ready.sem, xnT_ready.at(b, 1))
            for h in range(HA):
                for k in range(KT):
                    ins = nc.tensor.matmul(score[:, h // 4, (h % 4) * P:(h % 4 + 1) * P], wq_sb[:, k, h * DH:(h + 1) * DH],
                                           xnT[:, k], start=(k == 0), stop=(k == KT - 1))
            ins.then_inc(lat_done.sem, 1)
            for i in range(2 * GA):
                for k in range(KT):
                    ins = nc.tensor.matmul(score[0:DL, 2, i * P:(i + 1) * P],
                                           down[:, k, i // 2, (i % 2) * DL:(i % 2 + 1) * DL], xnT[:, k],
                                           start=(k == 0), stop=(k == KT - 1))
            ins.then_inc(lat_done.sem, 1)
            if not last:
                pe.wait_ge(clo_ready.sem, clo_ready.at(b + 1, 1))
                turn_context(b + 1, 1)
            pe.wait_ge(lat_ready.sem, lat_ready.at(b, 1))
            for g in range(GA):
                nc.tensor.matmul(score[:, 3, g * P:(g + 1) * P], up[:, 0], lat[:, g], start=True, stop=True)
            for g in range(GA):
                ins = nc.tensor.matmul(score[:, 3, (GA + g) * P:(GA + g + 1) * P], lat[:, GA + g], up[:, 1], start=True,
                                       stop=True)
            ins.then_inc(kva_done.sem, 1)
            pe.wait_ge(kva_ready.sem, kva_ready.at(b, 1))
            pe.wait_ge(qa_ready.sem, qa_ready.at(b, 1))
            for h in range(HA):
                ins = nc.tensor.matmul(score[:, h // 4, (h % 4) * P:(h % 4 + 1) * P], qT_a[:, h], kv_a[:, h // 4],
                                       start=True, stop=True)
            ins.then_inc(sb_done.sem, 1)
            if not last:
                pe.wait_ge(masked.sem, masked.at(b, 1))
                keys_and_values(b + 1, 0)
                pe.wait_ge(clo_ready.sem, clo_ready.at(b + 1, 2))
            pe.wait_ge(pb_normed.sem, pb_normed.at(b, 2))
            for h in range(HA):
                ins = nc.tensor.transpose(turnb[:, h // 4, (h % 4) * P:(h % 4 + 1) * P], prob_b[:, h], ident[:])
                if h % 4 == 3:
                    ins.then_inc(pTb_done.sem, 1)
            if not last:
                pe.wait_ge(k_ready.sem, k_ready.at(b + 1, 4))
                pe.wait_ge(v_ready.sem, v_ready.at(b + 1, 4))
            for g in range(GA):
                if g == 0:
                    pe.wait_ge(pTb_act.sem, pTb_act.at(b, 1))
                else:
                    pe.wait_ge(pTb_dve.sem, pTb_dve.at(b, 1))
                nc.tensor.matmul(score[:, 2 + g], kv_a[:, GA + g],
                                 probT_b[:, 4 * g:4 * g + 4].rearrange("p h t -> p (h t)"), start=True,
                                 stop=True).then_inc(ob_done.sem, 1)
            for h in range(HA):
                if h == 0:
                    pe.wait_ge(wo_loaded.sem, wo_loaded.at(b, 16))
                    pe.wait_ge(ob_act.sem, ob_act.at(b, 1))
                if h == 4:
                    pe.wait_ge(ob_dve.sem, ob_dve.at(b, 1))
                ins = nc.tensor.matmul(miscb[:], mixT_b[:, h], wo_sb[:, h], start=(h == 0), stop=(h == HA - 1))
            ins.then_inc(y_done.sem, 1)

        with pe.Fori(0, NB - 1) as b:
            batch(b, False)
        batch(NB - 1, True)


def local_transformer(nc, ctx, tabs, X, OUTER, shared, out_dram, w):
    Wqkv, q_scale, k_scale, Wo, ln_g, ln_b, W1, b1, W2, b2 = w
    DEPTH = Wqkv.shape[0]
    HEADS_HALF, DH = 8, 64
    INNER2 = W2.shape[1]
    FT = (INNER2 + P - 1) // P
    FTAIL = INNER2 - (FT - 1) * P

    chunk_names = [("qkv", 0, 0), ("qkv", 1, 0), ("qkv", 2, 0), ("qkv", 0, 1), ("qkv", 1, 1), ("qkv", 2, 1),
                   ("wo", 0), ("wo", 1)] + [("w1", c) for c in range(6)] + [("w2", c) for c in range(4)]
    assert chunk_names[:2] == list(CHUNKS_AHEAD)
    NCH = len(chunk_names)
    C_Q0, C_WO, C_W1, C_W2 = 0, 6, 8, 14
    QKV_UNITS = [(0, b) for b in range(NB)] + [(1, b) for b in range(NB)]
    QKV_UNITS += [(3, 0), (2, 0), (3, 1), (2, 1), (4, 0), (2, 2), (4, 1), (2, 3), (4, 2), (3, 2), (4, 3), (3, 3)]
    QKV_UNITS += [(5, b) for b in range(NB)]
    WO_UNITS = [(C_WO + h, b) for h, b in ((0, 0), (0, 1), (1, 0), (1, 1), (0, 2), (1, 2), (0, 3), (1, 3))]
    wo_no = {(c - C_WO, b): n for n, (c, b) in enumerate(WO_UNITS)}
    NQ, NO = len(QKV_UNITS), len(WO_UNITS)
    U_W1 = NQ + NO
    U_W2 = U_W1 + 2 * FT
    NU = U_W2 + NB
    rot_units = [u for u in range(NQ) if QKV_UNITS[u][0] % 3 != 2]
    rot_no = {u: n for n, u in enumerate(rot_units)}
    NROT = len(rot_units)
    v_units = [u for u in range(NQ) if u not in rot_no]
    v_no = {u: n for n, u in enumerate(v_units)}
    steps = [("turn_x", b) for b in range(NB)]
    def emit_unit(u):
        steps.append(("products", u))
        steps.extend((stage, v) for stage, v in (("rotate", u - 2), ("sum_squares", u - 1)) if v in rot_no)
        steps.append(("empty", u))
        if u - 1 in rot_no:
            steps.append(("invert", u - 1))

    for u in range(2 * NB):
        emit_unit(u)
    for a in range(2 * NB):
        steps.append(("turn_qk", a))
        if a >= 3:
            steps.append(("keep", a - 3))
        emit_unit(2 * NB + 2 * a)
        if a:
            steps.append(("divide", a - 1))
        if a >= 2:
            steps.append(("turn_p", a - 2))
        steps.append(("scores", a))
        emit_unit(2 * NB + 2 * a + 1)
        if a >= 2:
            steps.append(("values", a - 2))
    for s in (0, ("keep", 5), ("turn_p", 6), 1, ("divide", 7), 2, ("values", 6), 3, ("keep", 6), ("turn_p", 7),
              ("shift", 0), 4, ("values", 7), ("shift", 1), ("keep", 7), 5, ("turn_n", 0), 6, ("shift", 2),
              ("turn_n", 1), 7):
        if isinstance(s, int):
            emit_unit(NQ + s)
        else:
            steps.append(s)
    early = [("gate", 0), ("value", 0), ("gate", 1)]
    steps += [(k, f, 0) for k, f in early[:1]]
    steps.append(("shift", 3))
    steps += [(k, f, 0) for k, f in early[1:]]
    steps.append(("turn_n", 2))
    steps.append(("turn_n", 3))
    steps += [(k, f, 1) for k, f in early]
    for f in range(1, FT):
        if f > 1:
            steps.append(("gate", f, None))
        steps.append(("value", f, None))
    steps.append(("last_split", 0))
    for c in range(4):
        for b in range(NB):
            steps.append(("down", c, b))
    for b in range(NB):
        steps.append(("add_down", b))

    first_use, last_use = {}, {}

    def chunks_of(step):
        if step[0] == "products":
            u = step[1]
            return QKV_UNITS[u][0] if u < NQ else WO_UNITS[u - NQ][0]
        if step[0] == "gate" or step[0] == "value":
            return C_W1 + step[1] // 2
        if step[0] == "down":
            return C_W2 + step[1]
        return None

    for n, s in enumerate(steps):
        c = chunks_of(s)
        if c is not None:
            first_use.setdefault(c, n)
            last_use[c] = n
    split_at = {}
    start = 0
    for c in range(NCH):
        start, end = max(start, last_use.get(c - 1, -1) + 1), first_use.get(c + 2, len(steps))
        uses = [n for n, s in enumerate(steps) if chunks_of(s) is not None and start <= n < end]
        for t in range(4):
            start = uses[t * len(uses) // (8 if c not in (2, 3, 4, 5) else 6)]
            split_at.setdefault(start, []).append((c + 2, t))

    turns = []
    for s in steps:
        if s[0] == "turn_x" or s[0] == "turn_n":
            turns.append((s[0], s[1], 0))
        elif s[0] == "turn_qk" or s[0] == "turn_p":
            turns += [(s[0], s[1], 0), (s[0], s[1], 1)]
    turn_no = {t: n for n, t in enumerate(turns)}
    NTURN = len(turns)
    turn_act = {}
    turn_dve = {}
    for n, t in enumerate(turns):
        if t[0] == "turn_qk" and t[2] == 1 or t[0] == "turn_p" and t[2] == 0:
            turn_act[n] = len(turn_act)
        else:
            turn_dve[n] = len(turn_dve)
    assert all(n % 2 == t[2] for n, t in enumerate(turns) if t[0] in ("turn_qk", "turn_p")) and NTURN % 2 == 0

    def sb(name, shape, dt=F32):
        return ctx.enter_context(nc.sbuf_tensor(name, shape, dt))

    def ps(name, shape):
        return ctx.enter_context(nc.psum_tensor(name, shape, F32))

    def signal(name, per, first=0):
        return Signal(ctx.enter_context(nc.semaphore(name)), per, first)

    ident, shiftm, maskadd, rotary_dram = tabs

    whi, wlo, raw = ([t.rearrange("p (t n) -> p t n", t=4) for t in part] for part in shared)
    whi.append(sb("whi2", [P, 4, 512], F32R))
    wlo.append(sb("wlo2", [P, 4, 512], F32R))
    xt_hi = sb("xt_hi", [P, 4, NB * P], F32R)
    xt_lo = sb("xt_lo", [P, 4, NB * P], F32R)
    HID = FT * 512
    QKVW, ATW = 3 * NB * 512, 8 * 128 * 7 + 2 * 512
    region = sb("region", [P, QKVW + ATW])
    region_address = nc.sbuf_base - 4 * (QKVW + ATW)
    qrow = region[:, 0:NB * 512].rearrange("p (b n) -> p b n", b=NB)
    krow = region[:, NB * 512:2 * NB * 512].rearrange("p (b n) -> p b n", b=NB)
    vrow = region[:, 2 * NB * 512:3 * NB * 512].rearrange("p (b n) -> p b n", b=NB)
    at = QKVW
    qT = region[:, at:at + 1024].rearrange("p (s h t) -> p s h t", s=2, h=4)
    at += 1024
    prob = region[:, at:at + 3072].rearrange("p (s h t) -> p s h t", s=3, h=8)
    at += 3072
    probT = region[:, at:at + 2048].rearrange("p (s h t) -> p s h t", s=2, h=8)
    at += 2048
    assert at >= 2 * HID
    kD = region[:, at:at + 2048].rearrange("p (s h e t) -> p s h e t", s=2, h=4, e=2)
    where = region_address
    hid_hi = nc.alloc_sbuf_tensor_at("hid_hi", [P, FT, 512], F32R, offset=where)
    hid_lo = nc.alloc_sbuf_tensor_at("hid_lo", [P, FT, 512], F32R, offset=where + 4 * HID)
    mixT_hi = sb("mixT_hi", [P, 8, NB * P], F32R)
    mixT_lo = sb("mixT_lo", [P, 8, NB * P], F32R)
    sq = sb("sq", [P, 2, 512])
    wide_a = sb("wide_a", [P, 2, 512])
    wide_b = sb("wide_b", [P, 2, 512])
    straight, xn, hfull = wide_a, wide_a, wide_a
    turned_half, gate_out = wide_b, wide_b
    ss = sb("ss", [P, 2, 8])
    negmax = sb("negmax", [P, 2, 8])
    rowmax = sb("rowmax", [P, 8])
    psums = sb("psums", [P, 3, 8])
    rnorm = sb("rnorm", [P, NROT, 8])
    ident16 = sb("ident16", [P, P], mybir.dt.bfloat16)
    mask16 = sb("mask16", [P, P], mybir.dt.bfloat16)
    rsums = sb("rsums", [P, 2, 8])
    stats = sb("stats", [P, 12])
    meanvar = sb("meanvar", [P, 2, 2])
    rstd = sb("rstd", [P, 2])
    stats_seen = signal("stats_seen", NB)
    halfvar = sb("halfvar", [P, 2])
    lnbuf = sb("lnbuf", [P, 17])
    step_tmp = sb("step_tmp", [P, 8])
    half_log = sb("half_log", [P, 1])
    base_tab = sb("base_tab", [P, 4, DH])
    scales = sb("scales", [P, 2, DH])
    cur_tab = sb("cur_tab", [P, 4, DH])
    gB = sb("gB", [P, 512])
    bB = sb("bB", [P, 512])
    b2B = sb("b2B", [P, 512])
    b1T = sb("b1T", [P, 2 * FT])

    proj = [ps(f"proj{i}", [P, 512]) for i in range(3)]
    turnb = [ps(f"turnb{i}", [P, 512]) for i in range(2)]
    score = ps("score", [P, 8, P])
    mix = ps("mix", [P, 512])

    raw_loaded = [signal(f"raw_loaded{i}", 0, -16) for i in range(2)]
    tables_loaded = signal("tables_loaded", 0)
    scales_loaded = signal("scales_loaded", 2 * 16)
    layer_loaded = signal("layer_loaded", 0)
    hi_ready = signal("hi_ready", NCH, 2)
    lo_ready = signal("lo_ready", NCH, 2)
    down_used = signal("down_used", 3, 3)
    proj_done = signal("proj_done", NU, 1)
    v_ready = signal("v_ready", 2 * NB)
    x_added = signal("x_added", NO)
    gate_read = signal("gate_read", FT)
    turned = signal("turned", NTURN)
    turn_read_act = signal("turn_read_act", len(turn_act), 2)
    turn_read_dve = signal("turn_read_dve", len(turn_dve), 2)
    xhi_ready = signal("xhi_ready", 2 * NB)
    squared = signal("squared", NROT)
    sumsq_ready = signal("sumsq_ready", 2 * NROT, 3)
    logs_ready = signal("logs_ready", NROT + NB)
    newton_step = signal("newton_step", 3 * (NROT + NB))
    rnorm_ready = signal("rnorm_ready", NROT)
    copied = signal("copied", NROT)
    cosines = signal("cosines", NROT, 2)
    sines = signal("sines", NROT, 2)
    rotated = signal("rotated", NROT, 2)
    k_scaled = signal("k_scaled", 2 * NB)
    tabs_ready = signal("tabs_ready", 2, 1)
    scored = signal("scored", 8)
    max_ready = signal("max_ready", 8)
    negmax_ready = signal("negmax_ready", 8)
    probs_ready = signal("probs_ready", 8, 1)
    recip_ready = signal("recip_ready", 8)
    probs_normed = signal("probs_normed", 8)
    mix_done = signal("mix_done", 2 * NB)
    shifted = signal("shifted", NB)
    mixlo_ready = signal("mixlo_ready", 2 * NB)
    mixhi_ready = signal("mixhi_ready", 8)
    stats_ready = signal("stats_ready", 3 * NB)
    rstd_ready = signal("rstd_ready", NB)
    ln_normed = signal("ln_normed", NB)
    ln_centred = signal("ln_centred", NB)
    x_biased = signal("x_biased", NB)
    hidden_full = signal("hidden_full", FT)
    hidhi_ready = signal("hidhi_ready", FT)
    hidlo_ready = signal("hidlo_ready", FT)
    x_new = signal("x_new", NB, NB)
    zero_ready = signal("zero_ready", 0)
    sum_ready = signal("sum_ready", 0)
    stored = signal("stored", 0)

    dmas_of = [2 if name[0] == "w1" or name == ("w2", 3) else 1 for name in chunk_names]
    slot_total = [16 * sum(d for c, d in enumerate(dmas_of) if c % 2 == s) for s in range(2)]
    for s in range(2):
        raw_loaded[s].per = slot_total[s]

    def landed(c):
        return 16 * sum(d for k, d in enumerate(dmas_of[:c + 1]) if k % 2 == c % 2)

    LAYER_DMAS = 7
    layer_loaded.per = 16 * LAYER_DMAS

    def piece(buf, c, t):
        name = chunk_names[c]
        if name == ("w1", 5):
            return buf[:, t].rearrange("p (g n) -> p g n", g=2)[:, :, 0:FTAIL]
        if name[0] == "w2" and t == 3 or name == ("w2", 3) and t >= 2:
            return None
        if name == ("w2", 3) and t == 1:
            return buf[0:FTAIL, t, :]
        return buf[:, t, :]

    def npieces(c):
        return sum(piece(raw[0], c, t) is not None for t in range(4))

    def row(ap, l):
        return ap[bass.ds(l, 1)]

    block = ctx.enter_context(nc.Block())

    @block.sync
    def _(sp):
        sp.dma_start(base_tab[:], rotary_dram).then_inc(tables_loaded.sem, 16)

        def load(l, c):
            sp.wait_ge(lo_ready.sem, lo_ready.at(l, c - 1))
            name, buf, sem = chunk_names[c], raw[c % 2], raw_loaded[c % 2].sem
            if name[0] == "qkv":
                col = name[1] * 1024 + name[2] * 512
                src = row(Wqkv, l).rearrange("o (t p) n -> p (o t) n", p=P)[:, :, col:col + 512]
                sp.dma_start(buf, src).then_inc(sem, 16)
            elif name[0] == "wo":
                src = row(Wo, l).rearrange("o (t p) n -> p (o t) n", p=P)[:, 4 * name[1]:4 * name[1] + 4]
                sp.dma_start(buf, src).then_inc(sem, 16)
            elif name[0] == "w1":
                n = 256 if name[1] < 5 else FTAIL
                src = row(W1, l).rearrange("o (t p) n -> p (o t) n", p=P)
                for g, base in enumerate((INNER2, 0)):
                    col = base + 256 * name[1]
                    sp.dma_start(buf[:, :, 256 * g:256 * g + n], src[:, :, col:col + n]).then_inc(sem, 16)
            else:
                r0 = 3 * P * name[1]
                full = 3 if name[1] < 3 else 1
                src = row(W2, l).rearrange("o r n -> (o r) n")
                sp.dma_start(buf[:, 0:full], src[r0:r0 + full * P].rearrange("(t p) n -> p t n", p=P)).then_inc(sem, 16)
                if name[1] == 3:
                    sp.dma_start(buf[0:FTAIL, 1], src[r0 + P:r0 + P + FTAIL]).then_inc(sem, 16)

        def load_layer(l):
            sp.wait_ge(x_new.sem, x_new.at(l, 0))
            sem = layer_loaded.sem
            sp.dma_start(gB[:], row(ln_g, l).to_broadcast([P, 512])).then_inc(sem, 16)
            sp.dma_start(bB[:], row(ln_b, l).to_broadcast([P, 512])).then_inc(sem, 16)
            sp.dma_start(b2B[:], row(b2, l).to_broadcast([P, 512])).then_inc(sem, 16)
            bias = row(b1, l).rearrange("o n -> (o n)")
            for g, base in enumerate((INNER2, 0)):
                n = (FT - 1) * P
                sp.dma_start(b1T[:, g * FT:g * FT + FT - 1],
                             bias[base:base + n].rearrange("(f p) -> p f", p=P),
                             allow_slow_non_contiguous=True).then_inc(sem, 16)
                sp.dma_start(b1T[0:FTAIL, g * FT + FT - 1:g * FT + FT],
                             bias[base + n:base + n + FTAIL].rearrange("(p f) -> p f", f=1),
                             allow_slow_non_contiguous=True).then_inc(sem, 16)


        def layer(l, last):
            sp.wait_ge(tabs_ready.sem, tabs_ready.at(l, 0))
            for j, scale in enumerate((q_scale, k_scale)):
                sp.dma_start(scales[:, j], row(scale, l).to_broadcast([P, DH])).then_inc(scales_loaded.sem, 16)
            for c in range(2, NCH):
                if c == 4:
                    load_layer(l)
                load(l, c)
            if not last:
                load(l + 1, 0)
                load(l + 1, 1)

        with sp.Fori(0, DEPTH - 1) as l:
            layer(l, False)
        layer(DEPTH - 1, True)
        for b in range(NB):
            sp.wait_ge(sum_ready.sem, b + 1)
            sp.dma_start(out_dram[b], X[:, b]).then_inc(stored.sem, 16)
        sp.wait_ge(stored.sem, 16 * NB)

    def chunk_is_used(eng, l, c):
        back = c < 0
        c = c % NCH
        if C_W2 <= c < NCH - 1:
            eng.wait_ge(down_used.sem, down_used.at(l, c - C_W2 + 1 - (down_used.per if back else 0)))
            return
        step = steps[last_use[c]]
        u = {"products": lambda: step[1], "gate": lambda: U_W1 + 2 * step[1], "value": lambda: U_W1 + 2 * step[1] + 1,
             "down": lambda: NU - 1}[step[0]]()
        eng.wait_ge(proj_done.sem, proj_done.at(l, u + 1 - (NU if back else 0)))

    def split_hi(act, l, c):
        chunk_is_used(act, l, c - 3)
        act.wait_ge(raw_loaded[c % 2].sem, raw_loaded[c % 2].at(l, landed(c)))
        n = npieces(c)
        for t in range(n):
            if chunk_names[c][0] == "w1" and chunk_names[c][1] == 5 or chunk_names[c] == ("w2", 3):
                ins = nc.scalar.copy(piece(whi[c % 3], c, t), piece(raw[c % 2], c, t))
            elif t == 0:
                ins = nc.scalar.copy(whi[c % 3][:, 0:n], raw[c % 2][:, 0:n])
        ins.then_inc(hi_ready.sem, 1)

    def split_lo(pool, l, c, t):
        if piece(raw[0], c, t) is None:
            return
        if t == 0:
            pool.wait_ge(hi_ready.sem, hi_ready.at(l, c + 1))
        ins = nc.gpsimd.tensor_tensor(piece(wlo[c % 3], c, t), piece(raw[c % 2], c, t), piece(whi[c % 3], c, t),
                                      ALU.subtract)
        if t == npieces(c) - 1:
            ins.then_inc(lo_ready.sem, 1)

    def splits(n, l, last):
        for c, t in split_at.get(n, []):
            if c < NCH:
                yield l, c, t
            elif not last:
                yield l + 1, c - NCH, t

    def is_q(u):
        return QKV_UNITS[u][0] % 3 == 0

    def q_unit(a):
        return rot_no[QKV_UNITS.index((a // NB * 3, a % NB))]

    def kind_no(u):
        return sum(is_q(v) == is_q(u) for v in rot_units if v < u)

    def shift_bank(b):
        return score[:, 4 * (b % 2):4 * (b % 2) + 2].rearrange("p h t -> p (h t)")

    def whole(s):
        return len(s) < 3 or s[2] != 0

    def rot_buf(u):
        c, b = QKV_UNITS[u]
        return (qrow, krow)[c % 3][:, b]

    @block.scalar
    def _(act):
        nc.scalar.sem_inc(hi_ready.sem, 4)
        nc.scalar.sem_inc(probs_ready.sem, 1)
        nc.scalar.sem_inc(turn_read_act.sem, 2)

        def layer(l, last):
            nc.scalar.preload_act_table_set(LN_EXP_SET)
            for n, s in enumerate(steps):
                for ll, c, t in splits(n, l, last):
                    if t == 0:
                        split_hi(act, ll, c)
                k = s[0]
                if k == "turn_x" or k == "turn_n":
                    b = s[1]
                    e = turn_no[(k, b, 0)]
                    act.wait_ge(turned.sem, turned.at(l, e + 1))
                    nc.scalar.copy(xt_hi[:, :, b * P:(b + 1) * P],
                                   turnb[e % 2].rearrange("p (k t) -> p k t", k=4)).then_inc(xhi_ready.sem, 1)
                elif k == "empty" and s[1] in rot_no:
                    u = s[1]
                    r = rot_no[u]
                    act.wait_ge(cosines.sem, cosines.at(l, r - 1))
                    act.wait_ge(sines.sem, sines.at(l, r - 1))
                    act.wait_ge(proj_done.sem, proj_done.at(l, u + 1))
                    nc.scalar.copy(straight[:, r % 2], proj[u % 3][:]).then_inc(copied.sem, 1)
                    act.wait_ge(sumsq_ready.sem, sumsq_ready.at(l, 2 * r - 2))
                    nc.scalar.activation(sq[:, r % 2], proj[u % 3][:], ACT.Square).then_inc(squared.sem, 1)
                elif k == "invert":
                    r = rot_no[s[1]]
                    act.wait_ge(sumsq_ready.sem, sumsq_ready.at(l, 2 * r + 2))
                    nc.scalar.activation(lnbuf[:, 8 * (r % 2):8 * (r % 2) + 8], ss[:, r % 2], ACT.Ln,
                                         scale=-2.0 * LN_SHIFT).then_inc(logs_ready.sem, 1)
                    act.wait_ge(logs_ready.sem, logs_ready.at(l, r + 1))
                    nc.scalar.activation(rnorm[:, r], lnbuf[:, 8 * (r % 2):8 * (r % 2) + 8], ACT.Exp, bias=half_log[:, 0:1],
                                         scale=-0.5).then_inc(rnorm_ready.sem, 1)
                elif k == "shift":
                    b = s[1]
                    act.wait_ge(stats_ready.sem, stats_ready.at(l, 3 * b + 3))
                    nc.scalar.activation(lnbuf[:, 16:17], halfvar[:, b % 2:b % 2 + 1], ACT.Ln,
                                         scale=-2.0).then_inc(logs_ready.sem, 1)
                    act.wait_ge(logs_ready.sem, logs_ready.at(l, NROT + b + 1))
                    nc.scalar.activation(rstd[:, b % 2:b % 2 + 1], lnbuf[:, 16:17], ACT.Exp,
                                         scale=-0.5).then_inc(rstd_ready.sem, 1)
                elif k == "turn_qk":
                    a = s[1]
                    e = turn_no[(k, a, 1)]
                    if a == 0:
                        act.wait_ge(zero_ready.sem, 1)
                    act.wait_ge(turned.sem, turned.at(l, e + 1))
                    src = turnb[1].rearrange("p (h t) -> p h t", h=4)
                    nc.scalar.copy(kD[0:64, a % 2, :, 0, :], src[0:64])
                    nc.scalar.copy(kD[64:128, a % 2, :, 1, :], src[64:128]).then_inc(turn_read_act.sem, 1)
                elif k == "scores":
                    a = s[1]
                    act.wait_ge(negmax_ready.sem, negmax_ready.at(l, a + 1))
                    for h in range(8):
                        ins = nc.scalar.activation(prob[:, a % 3, h], score[:, h], ACT.Exp,
                                                   bias=negmax[:, a % 2, h:h + 1], scale=rnorm[:, q_unit(a), h:h + 1],
                                                   accum_out=psums[:, a % 3, h:h + 1])
                    ins.then_inc(probs_ready.sem, 1)
                elif k == "turn_p":
                    a = s[1]
                    e = turn_no[(k, a, 0)]
                    act.wait_ge(turned.sem, turned.at(l, e + 1))
                    nc.scalar.copy(probT[:, a % 2, 0:4],
                                   turnb[0].rearrange("p (h t) -> p h t", h=4)).then_inc(turn_read_act.sem, 1)
                elif k == "keep":
                    a = s[1]
                    b, hf = a % NB, a // NB
                    act.wait_ge(mix_done.sem, mix_done.at(l, a + 1))
                    nc.scalar.copy(mixT_hi[:, 4 * hf:4 * hf + 4, b * P:(b + 1) * P],
                                   mix.rearrange("p (h t) -> p h t", h=4)).then_inc(mixhi_ready.sem, 1)
                elif k == "gate" and whole(s):
                    f = s[1]
                    rows = P if f < FT - 1 else FTAIL
                    if f == 0:
                        act.wait_ge(layer_loaded.sem, layer_loaded.at(l, 16 * LAYER_DMAS))
                    if f >= 2:
                        act.wait_ge(hidden_full.sem, hidden_full.at(l, f - 1))
                    u = U_W1 + 2 * f
                    act.wait_ge(proj_done.sem, proj_done.at(l, u + 1))
                    nc.scalar.activation(gate_out[0:rows, f % 2], proj[u % 3][0:rows], ACT.Gelu,
                                         bias=b1T[0:rows, f:f + 1]).then_inc(gate_read.sem, 1)
                    if f:
                        hidden_high(act, l, f - 1)
                elif k == "last_split":
                    hidden_high(act, l, FT - 1)

        def hidden_high(act, l, f):
            rows = P if f < FT - 1 else FTAIL
            act.wait_ge(hidden_full.sem, hidden_full.at(l, f + 1))
            nc.scalar.copy(hid_hi[0:rows, f], hfull[0:rows, f % 2]).then_inc(hidhi_ready.sem, 1)

        with act.Fori(0, DEPTH - 1) as l:
            layer(l, False)
        layer(DEPTH - 1, True)

    @block.gpsimd
    def _(pool):
        nc.gpsimd.sem_inc(lo_ready.sem, 4)
        nc.gpsimd.sem_inc(sines.sem, 2)
        nc.gpsimd.sem_inc(tabs_ready.sem, 1)
        nc.gpsimd.tensor_copy(ident16[:], ident[:])
        nc.gpsimd.tensor_copy(mask16[:], maskadd[:])
        nc.gpsimd.memset(kD[:], 0.0).then_inc(zero_ready.sem, 1)
        pool.wait_ge(tables_loaded.sem, 16)

        def layer(l, last):
            pool.wait_ge(rotated.sem, rotated.at(l, 0))
            pool.wait_ge(scales_loaded.sem, scales_loaded.at(l, 32))
            for j in range(4):
                ins = nc.gpsimd.tensor_tensor(cur_tab[:, j], base_tab[:, j],
                                              scales[:, j // 2], ALU.mult)
            ins.then_inc(tabs_ready.sem, 2)
            pool.wait_ge(tabs_ready.sem, tabs_ready.at(l, 2))
            for n, s in enumerate(steps):
                k = s[0]
                if k == "rotate" and not is_q(s[1]):
                    u = s[1]
                    r = rot_no[u]
                    pool.wait_ge(rotated.sem, rotated.at(l, r + 1))
                    pool.wait_ge(newton_step.sem, newton_step.at(l, 3 * r + 3))
                    nc.gpsimd.tensor_tensor(rot_buf(u).rearrange("p (h d) -> p h d", h=8),
                                            rot_buf(u).rearrange("p (h d) -> p h d", h=8),
                                            rnorm[:, r].unsqueeze(2).to_broadcast([P, 8, DH]),
                                            ALU.mult).then_inc(k_scaled.sem, 1)
                elif k == "empty" and s[1] in rot_no:
                    u = s[1]
                    r = rot_no[u]
                    pool.wait_ge(rotated.sem, rotated.at(l, r - 1))
                    pool.wait_ge(copied.sem, copied.at(l, r + 1))
                    j = 1 if is_q(u) else 3
                    nc.gpsimd.tensor_tensor(turned_half[:, r % 2].rearrange("p (h d) -> p h d", h=8),
                                            straight[:, r % 2].rearrange("p (h d) -> p h d", h=8),
                                            cur_tab[:, j:j + 1].to_broadcast([P, 8, DH]),
                                            ALU.mult).then_inc(sines.sem, 1)
                elif k == "divide":
                    a = s[1]
                    pool.wait_ge(recip_ready.sem, recip_ready.at(l, a + 1))
                    nc.gpsimd.tensor_tensor(prob[:, a % 3], prob[:, a % 3],
                                            rsums[:, a % 2].unsqueeze(2).to_broadcast([P, 8, P]),
                                            ALU.mult).then_inc(probs_normed.sem, 1)
                elif k == "gate" and s[1] in (2, 4, 6, 8):
                    b = s[1] // 2 - 1
                    nc.gpsimd.tensor_tensor(X[:, b], X[:, b], b2B[:], ALU.add).then_inc(x_biased.sem, 1)
                for ll, c, t in splits(n, l, last):
                    split_lo(pool, ll, c, t)

        with pool.Fori(0, DEPTH - 1) as l:
            layer(l, False)
        layer(DEPTH - 1, True)

    @block.vector
    def _(dve):
        nc.vector.memset(half_log[:], float(0.5 * np.log(LN_SHIFT)))
        nc.vector.sem_inc(turn_read_dve.sem, 2)
        nc.vector.sem_inc(sumsq_ready.sem, 3)
        nc.vector.sem_inc(cosines.sem, 2)
        nc.vector.sem_inc(rotated.sem, 2)
        nc.vector.sem_inc(x_new.sem, NB)

        def layer(l, last):
            for n, s in enumerate(steps):
                k = s[0]
                if k == "turn_x" or k == "turn_n":
                    b = s[1]
                    e = turn_no[(k, b, 0)]
                    j = b if k == "turn_x" else NB + b
                    dve.wait_ge(xhi_ready.sem, xhi_ready.at(l, j + 1))
                    nc.vector.tensor_tensor(xt_lo[:, :, b * P:(b + 1) * P],
                                            turnb[e % 2].rearrange("p (k t) -> p k t", k=4),
                                            xt_hi[:, :, b * P:(b + 1) * P].bitcast(F32),
                                            ALU.subtract).then_inc(turn_read_dve.sem, 1)
                elif k == "empty" and s[1] in rot_no:
                    u = s[1]
                    r = rot_no[u]
                    if r == 0:
                        dve.wait_ge(tabs_ready.sem, tabs_ready.at(l, 2))
                    dve.wait_ge(copied.sem, copied.at(l, r + 1))
                    j = 0 if is_q(u) else 2
                    nc.vector.tensor_tensor(rot_buf(u).rearrange("p (h d) -> p h d", h=8),
                                            straight[:, r % 2].rearrange("p (h d) -> p h d", h=8),
                                            cur_tab[:, j:j + 1].to_broadcast([P, 8, DH]),
                                            ALU.mult).then_inc(cosines.sem, 1)
                elif k == "sum_squares":
                    r = rot_no[s[1]]
                    dve.wait_ge(squared.sem, squared.at(l, r + 1))
                    nc.vector.tensor_reduce(ss[:, r % 2], sq[:, r % 2].rearrange("p (h d) -> p h d", h=8), AX.X,
                                            ALU.add).then_inc(sumsq_ready.sem, 1)
                    dve.wait_ge(sumsq_ready.sem, sumsq_ready.at(l, 2 * r + 1))
                    nc.vector.tensor_scalar(ss[:, r % 2], ss[:, r % 2], 1e-24, -0.5, ALU.max,
                                            ALU.mult).then_inc(sumsq_ready.sem, 1)
                elif k == "rotate":
                    u = s[1]
                    r = rot_no[u]
                    dve.wait_ge(rnorm_ready.sem, rnorm_ready.at(l, r + 1))
                    step = newton_steps(l, rnorm[:, r], ss[:, r % 2], r)
                    next(step)
                    dve.wait_ge(cosines.sem, cosines.at(l, r + 1))
                    dve.wait_ge(sines.sem, sines.at(l, r + 1))
                    q4 = rot_buf(u).rearrange("p (h s d) -> p h s d", h=8, s=2)
                    t4 = turned_half[:, r % 2].rearrange("p (h s d) -> p h s d", h=8, s=2)
                    nc.vector.tensor_tensor(q4[:, :, 0], q4[:, :, 0], t4[:, :, 1], ALU.add)
                    next(step)
                    nc.vector.tensor_tensor(q4[:, :, 1], q4[:, :, 1], t4[:, :, 0], ALU.add).then_inc(rotated.sem, 1)
                    next(step)
                elif k == "empty" and s[1] < NQ:
                    u = s[1]
                    dve.wait_ge(proj_done.sem, proj_done.at(l, u + 1))
                    nc.vector.tensor_copy(vrow[:, QKV_UNITS[u][1]], proj[u % 3][:]).then_inc(v_ready.sem, 1)
                elif k == "empty":
                    u = s[1]
                    hf, b = WO_UNITS[u - NQ][0] - C_WO, WO_UNITS[u - NQ][1]
                    dve.wait_ge(proj_done.sem, proj_done.at(l, u + 1))
                    if hf:
                        dve.wait_ge(x_added.sem, x_added.at(l, wo_no[(0, b)] + 1))
                    nc.vector.tensor_tensor(X[:, b], proj[u % 3][:], X[:, b], ALU.add).then_inc(x_added.sem, 1)
                elif k == "turn_qk":
                    a = s[1]
                    e = turn_no[(k, a, 0)]
                    dve.wait_ge(turned.sem, turned.at(l, e + 1))
                    nc.vector.tensor_copy(qT[:, a % 2],
                                          turnb[0].rearrange("p (h t) -> p h t", h=4)).then_inc(turn_read_dve.sem, 1)
                elif k == "scores":
                    a = s[1]
                    dve.wait_ge(scored.sem, scored.at(l, a + 1))
                    nc.vector.tensor_reduce(rowmax[:], score[:], AX.X, ALU.max).then_inc(max_ready.sem, 1)
                    dve.wait_ge(max_ready.sem, max_ready.at(l, a + 1))
                    dve.wait_ge(newton_step.sem, newton_step.at(l, 3 * q_unit(a) + 3))
                    nc.vector.scalar_tensor_tensor(out=negmax[:, a % 2], in0=rowmax[:], scalar=-1.0,
                                                   in1=rnorm[:, q_unit(a)], op0=ALU.mult,
                                                   op1=ALU.mult).then_inc(negmax_ready.sem, 1)
                elif k == "divide":
                    a = s[1]
                    dve.wait_ge(probs_ready.sem, probs_ready.at(l, a + 1))
                    nc.vector.reciprocal(rsums[:, a % 2], psums[:, a % 3]).then_inc(recip_ready.sem, 1)
                elif k == "turn_p":
                    a = s[1]
                    e = turn_no[(k, a, 1)]
                    dve.wait_ge(turned.sem, turned.at(l, e + 1))
                    nc.vector.tensor_copy(probT[:, a % 2, 4:8],
                                          turnb[1].rearrange("p (h t) -> p h t", h=4)).then_inc(turn_read_dve.sem, 1)
                elif k == "keep":
                    a = s[1]
                    b, hf = a % NB, a // NB
                    dve.wait_ge(mixhi_ready.sem, mixhi_ready.at(l, a + 1))
                    rng = mixT_hi[:, 4 * hf:4 * hf + 4, b * P:(b + 1) * P]
                    nc.vector.tensor_tensor(mixT_lo[:, 4 * hf:4 * hf + 4, b * P:(b + 1) * P],
                                            mix.rearrange("p (h t) -> p h t", h=4), rng.bitcast(F32),
                                            ALU.subtract).then_inc(mixlo_ready.sem, 1)
                elif k == "shift":
                    b = s[1]
                    dve.wait_ge(x_added.sem, x_added.at(l, wo_no[(1, b)] + 1))
                    nc.vector.bn_stats(stats[:, 0:6], X[:, b, 0:256])
                    dve.wait_ge(shifted.sem, shifted.at(l, b + 1))
                    nc.vector.bn_stats(stats[:, 6:12], shift_bank(b)).then_inc(stats_ready.sem, 1)
                    dve.wait_ge(stats_ready.sem, stats_ready.at(l, 3 * b + 1))
                    nc.vector.sem_inc(stats_seen.sem, 1)
                    nc.vector.bn_aggr(meanvar[:, b % 2], stats[:]).then_inc(stats_ready.sem, 1)
                    dve.wait_ge(stats_ready.sem, stats_ready.at(l, 3 * b + 2))
                    nc.vector.tensor_scalar(halfvar[:, b % 2:b % 2 + 1], meanvar[:, b % 2, 1:2], 1e-5, -0.5, ALU.add,
                                            ALU.mult).then_inc(stats_ready.sem, 1)
                    if b >= 2:
                        dve.wait_ge(turned.sem, turned.at(l, turn_no[("turn_n", b - 2, 0)] + 1))
                    if b == 0:
                        dve.wait_ge(layer_loaded.sem, layer_loaded.at(l, 16 * LAYER_DMAS))
                    for h, src in enumerate((X[:, b, 0:256], shift_bank(b))):
                        ins = nc.vector.scalar_tensor_tensor(
                            out=xn[:, b % 2, 256 * h:256 * h + 256], in0=src, scalar=meanvar[:, b % 2, 0:1],
                            in1=gB[:, 256 * h:256 * h + 256], op0=ALU.subtract, op1=ALU.mult)
                    ins.then_inc(ln_centred.sem, 1)
                    dve.wait_ge(rstd_ready.sem, rstd_ready.at(l, b + 1))
                    for _ in newton_steps(l, rstd[:, b % 2:b % 2 + 1], halfvar[:, b % 2:b % 2 + 1], NROT + b):
                        pass
                    dve.wait_ge(newton_step.sem, newton_step.at(l, 3 * (NROT + b) + 3))
                    dve.wait_ge(ln_centred.sem, ln_centred.at(l, b + 1))
                    nc.vector.scalar_tensor_tensor(out=xn[:, b % 2], in0=xn[:, b % 2],
                                                   scalar=rstd[:, b % 2:b % 2 + 1], in1=bB[:], op0=ALU.mult,
                                                   op1=ALU.add).then_inc(ln_normed.sem, 1)
                elif k == "value" and whole(s):
                    f = s[1]
                    rows = P if f < FT - 1 else FTAIL
                    u = U_W1 + 2 * f + 1
                    dve.wait_ge(gate_read.sem, gate_read.at(l, f + 1))
                    if f >= 2:
                        dve.wait_ge(hidlo_ready.sem, hidlo_ready.at(l, f - 1))
                    dve.wait_ge(proj_done.sem, proj_done.at(l, u + 1))
                    nc.vector.scalar_tensor_tensor(out=hfull[0:rows, f % 2], in0=proj[u % 3][0:rows],
                                                   scalar=b1T[0:rows, FT + f:FT + f + 1], in1=gate_out[0:rows, f % 2],
                                                   op0=ALU.add, op1=ALU.mult).then_inc(hidden_full.sem, 1)
                    if f:
                        hidden_low(l, f - 1)
                elif k == "last_split":
                    hidden_low(l, FT - 1)
                elif k == "add_down":
                    b = s[1]
                    u = U_W2 + b
                    dve.wait_ge(x_biased.sem, x_biased.at(l, b + 1))
                    dve.wait_ge(proj_done.sem, proj_done.at(l, u + 1))
                    src = proj[u % 3] if b < 3 else mix
                    nc.vector.tensor_tensor(X[:, b], src[:], X[:, b], ALU.add).then_inc(x_new.sem, 1)

        def newton_steps(l, y, minus_half, no):
            t = step_tmp[:, 0:y.shape[1]]
            yield nc.vector.tensor_tensor(t, y, y, ALU.mult).then_inc(newton_step.sem, 1)
            dve.wait_ge(newton_step.sem, newton_step.at(l, 3 * no + 1))
            yield nc.vector.tensor_tensor(t, t, minus_half, ALU.mult).then_inc(newton_step.sem, 1)
            dve.wait_ge(newton_step.sem, newton_step.at(l, 3 * no + 2))
            yield nc.vector.scalar_tensor_tensor(out=y, in0=t, scalar=1.5, in1=y, op0=ALU.add,
                                                 op1=ALU.mult).then_inc(newton_step.sem, 1)

        def hidden_low(l, f):
            rows = P if f < FT - 1 else FTAIL
            dve.wait_ge(hidhi_ready.sem, hidhi_ready.at(l, f + 1))
            nc.vector.tensor_tensor(hid_lo[0:rows, f], hfull[0:rows, f % 2], hid_hi[0:rows, f].bitcast(F32),
                                    ALU.subtract).then_inc(hidlo_ready.sem, 1)

        with dve.Fori(0, DEPTH - 1) as l:
            layer(l, False)
        layer(DEPTH - 1, True)
        for b in range(NB):
            dve.wait_ge(x_new.sem, x_new.at(DEPTH - 1, b + 1))
            nc.vector.tensor_tensor(X[:, b], X[:, b], OUTER[:, b], ALU.add).then_inc(sum_ready.sem, 1)

    @block.tensor
    def _(pe):
        nc.tensor.sem_inc(down_used.sem, 3)
        nc.tensor.sem_inc(proj_done.sem, 1)

        def bank_free(l, u):
            v = u - 3
            if v < 0:
                pe.wait_ge(x_new.sem, x_new.at(l, u + 1 - NB))
            elif v in rot_no:
                pe.wait_ge(squared.sem, squared.at(l, rot_no[v] + 1))
            elif v < NQ:
                pe.wait_ge(v_ready.sem, v_ready.at(l, v_no[v] + 1))
            elif v < U_W1:
                pe.wait_ge(x_added.sem, x_added.at(l, v - NQ + 1))
            elif (v - U_W1) % 2 == 0:
                pe.wait_ge(gate_read.sem, gate_read.at(l, (v - U_W1) // 2 + 1))
            else:
                pe.wait_ge(hidden_full.sem, hidden_full.at(l, (v - U_W1) // 2 + 1))

        def turn_bank_free(l, e):
            v = e - 2
            back = v < 0
            if back:
                v += NTURN
            if v in turn_act:
                pe.wait_ge(turn_read_act.sem, turn_read_act.at(l, turn_act[v] + 1 - (len(turn_act) if back else 0)))
            else:
                pe.wait_ge(turn_read_dve.sem, turn_read_dve.at(l, turn_dve[v] + 1 - (len(turn_dve) if back else 0)))

        def three_passes(dst, lhs, rhs, first, last):
            (lh, ll), (rh, rl) = lhs, rhs
            nc.tensor.matmul(dst, lh, rh, start=first, stop=False)
            nc.tensor.matmul(dst, lh, rl, start=False, stop=False)
            return nc.tensor.matmul(dst, ll, rh, start=False, stop=last)

        def layer(l, last):
            for n, s in enumerate(steps):
                k = s[0]
                c = chunks_of(s)
                if c is not None and first_use[c] == n:
                    pe.wait_ge(lo_ready.sem, lo_ready.at(l, c + 1))
                if k == "turn_x":
                    b = s[1]
                    e = turn_no[(k, b, 0)]
                    turn_bank_free(l, e)
                    pe.wait_ge(x_new.sem, x_new.at(l, b + 1 - NB))
                    for kt in range(4):
                        dst = turnb[e % 2][:, kt * P:(kt + 1) * P]
                        src = X[:, b, kt * P:(kt + 1) * P]
                        if kt < 2:
                            ins = nc.tensor.transpose(dst, src, ident[:])
                        else:
                            ins = nc.tensor.matmul(dst, src, shiftm[:], start=True, stop=True)
                    ins.then_inc(turned.sem, 1)
                elif k == "products":
                    u = s[1]
                    cc, b = QKV_UNITS[u] if u < NQ else WO_UNITS[u - NQ]
                    if u < NB:
                        pe.wait_ge(turn_read_dve.sem, turn_read_dve.at(l, turn_dve[turn_no[("turn_x", b, 0)]] + 1))
                    if u >= NQ:
                        hf = cc - C_WO
                        pe.wait_ge(mixlo_ready.sem, mixlo_ready.at(l, hf * NB + b + 1))
                    bank_free(l, u)
                    for kt in range(4):
                        if u < NQ:
                            lhs = tuple(x[:, kt, b * P:(b + 1) * P] for x in (xt_hi, xt_lo))
                        else:
                            lhs = tuple(x[:, 4 * hf + kt, b * P:(b + 1) * P] for x in (mixT_hi, mixT_lo))
                        rhs = tuple(x[cc % 3][:, kt] for x in (whi, wlo))
                        ins = three_passes(proj[u % 3][:], lhs, rhs, kt == 0, kt == 3)
                    ins.then_inc(proj_done.sem, 1)
                elif k == "turn_qk":
                    a = s[1]
                    b, hf = a % NB, a // NB
                    pe.wait_ge(rotated.sem, rotated.at(l, q_unit(a) + 1))
                    pe.wait_ge(k_scaled.sem, k_scaled.at(l, kind_no(QKV_UNITS.index((3 * hf + 1, b))) + 1))
                    for g, rows in enumerate((qrow, krow)):
                        e = turn_no[(k, a, g)]
                        turn_bank_free(l, e)
                        for h in range(4):
                            ins = nc.tensor.transpose(turnb[g][:, h * P:(h + 1) * P], rows[:, b, h * P:(h + 1) * P],
                                                      ident[:])
                        ins.then_inc(turned.sem, 1)
                elif k == "scores":
                    a = s[1]
                    pe.wait_ge(zero_ready.sem, zero_ready.at(0, 1))
                    pe.wait_ge(probs_ready.sem, probs_ready.at(l, a))
                    for g in range(2):
                        nc.tensor.matmul(score[:, 4 * g:4 * g + 4], ident16[:],
                                         mask16[:, :].unsqueeze(1).to_broadcast([P, 4, P]), start=True, stop=False)
                    pe.wait_ge(turn_read_dve.sem, turn_read_dve.at(l, turn_dve[turn_no[("turn_qk", a, 0)]] + 1))
                    pe.wait_ge(turn_read_act.sem, turn_read_act.at(l, turn_act[turn_no[("turn_qk", a, 1)]] + 1))
                    for h in range(4):
                        ins = nc.tensor.matmul(score[:, 2 * h:2 * h + 2].rearrange("p h t -> p (h t)"), qT[:, a % 2, h],
                                               kD[:, a % 2, h].rearrange("p e t -> p (e t)"), start=False, stop=h % 2 == 1)
                    ins.then_inc(scored.sem, 1)
                elif k == "turn_p":
                    a = s[1]
                    pe.wait_ge(probs_normed.sem, probs_normed.at(l, a + 1))
                    for g in range(2):
                        turn_bank_free(l, turn_no[(k, a, g)])
                        for h in range(4):
                            ins = nc.tensor.transpose(turnb[g][:, h * P:(h + 1) * P], prob[:, a % 3, 4 * g + h],
                                                      ident[:])
                        ins.then_inc(turned.sem, 1)
                elif k == "values":
                    a = s[1]
                    b = a % NB
                    uv = QKV_UNITS.index((3 * (a // NB) + 2, b))
                    pe.wait_ge(v_ready.sem, v_ready.at(l, v_no[uv] + 1))
                    if a:
                        pe.wait_ge(mixlo_ready.sem, mixlo_ready.at(l, a))
                    else:
                        pe.wait_ge(x_new.sem, x_new.at(l, 0))
                    pe.wait_ge(turn_read_act.sem, turn_read_act.at(l, turn_act[turn_no[("turn_p", a, 0)]] + 1))
                    for h in range(8):
                        if h == 4:
                            pe.wait_ge(turn_read_dve.sem, turn_read_dve.at(l, turn_dve[turn_no[("turn_p", a, 1)]] + 1))
                        r = 64 * (h % 2)
                        ins = nc.tensor.matmul(mix[r:r + 64, (h // 2) * P:(h // 2 + 1) * P],
                                               vrow[:, b, h * DH:(h + 1) * DH], probT[:, a % 2, h], start=True, stop=True)
                    ins.then_inc(mix_done.sem, 1)
                elif k == "shift":
                    b = s[1]
                    if b < 2:
                        pe.wait_ge(probs_ready.sem, probs_ready.at(l, 2 * NB))
                    else:
                        pe.wait_ge(ln_centred.sem, ln_centred.at(l, b - 1))
                    pe.wait_ge(x_added.sem, x_added.at(l, wo_no[(1, b)] + 1))
                    nc.tensor.matmul(shift_bank(b), shiftm[:], X[:, b, 256:512], start=True,
                                     stop=True).then_inc(shifted.sem, 1)
                elif k == "turn_n":
                    b = s[1]
                    e = turn_no[(k, b, 0)]
                    turn_bank_free(l, e)
                    pe.wait_ge(ln_normed.sem, ln_normed.at(l, b + 1))
                    for kt in range(4):
                        ins = nc.tensor.transpose(turnb[e % 2][:, kt * P:(kt + 1) * P],
                                                  xn[:, b % 2, kt * P:(kt + 1) * P], ident[:])
                    ins.then_inc(turned.sem, 1)
                elif k == "gate" or k == "value":
                    f = s[1]
                    g = 0 if k == "gate" else 1
                    u = U_W1 + 2 * f + g
                    rows = P if f < FT - 1 else FTAIL
                    col = 256 * g + P * (f % 2)
                    bs = {0: (0, NB // 2), 1: (NB // 2, NB), None: (0, NB)}[s[2]]
                    if f == 0 and g == 0:
                        pe.wait_ge(turn_read_dve.sem,
                                   turn_read_dve.at(l, turn_dve[turn_no[("turn_n", bs[1] - 1, 0)]] + 1))
                    if s[2] != 1:
                        bank_free(l, u)
                    span = slice(bs[0] * P, bs[1] * P)
                    for kt in range(4):
                        lhs = tuple(x[c % 3][:, kt, col:col + rows] for x in (whi, wlo))
                        ins = three_passes(proj[u % 3][0:rows, span], lhs, (xt_hi[:, kt, span], xt_lo[:, kt, span]),
                                           kt == 0, kt == 3)
                    if s[2] != 0:
                        ins.then_inc(proj_done.sem, 1)
                elif k == "down":
                    _, cc, b = s
                    u = U_W2 + b
                    if cc == 0:
                        if b < 3:
                            bank_free(l, u)
                        else:
                            pe.wait_ge(mixlo_ready.sem, mixlo_ready.at(l, 2 * NB))
                    dst = proj[u % 3] if b < 3 else mix
                    for t in range(npieces(c)):
                        f = 3 * cc + t
                        if b == 0:
                            pe.wait_ge(hidlo_ready.sem, hidlo_ready.at(l, f + 1))
                        rows = P if f < FT - 1 else FTAIL
                        lhs = tuple(x[0:rows, f, b * P:(b + 1) * P] for x in (hid_hi, hid_lo))
                        rhs = tuple(x[c % 3][0:rows, t] for x in (whi, wlo))
                        ins = three_passes(dst[:], lhs, rhs, f == 0, f == FT - 1)
                    if f == FT - 1:
                        ins.then_inc(proj_done.sem, 1)
                    elif b == NB - 1:
                        ins.then_inc(down_used.sem, 1)
        with pe.Fori(0, DEPTH - 1) as l:
            layer(l, False)
        layer(DEPTH - 1, True)


_X = ["Wq", "bq", "Wk", "bk", "Wv", "bv", "Wo", "bo"]
_A = ["wq", "wk_down", "wv_down", "wk_up", "wv_up", "wo"]
_F = ["Wqkv", "q_scale", "k_scale", "Wo", "ln_g", "ln_b", "W1", "b1", "W2", "b2"]
_INS = (["x", "ctx_512"] + ["L0_xattn_" + n for n in _X] + ["L0_attn_" + n for n in _A] + ["L0_ffn_" + n for n in _F])


def perceiver_block(nc, ins, out):
    with ExitStack() as ctx:
        def sb(name, shape):
            return ctx.enter_context(nc.sbuf_tensor(name, shape, F32))

        X = sb("X", [P, NB, 512])
        OUTER = sb("OUTER", [P, NB, 512])
        shared = [[ctx.enter_context(nc.sbuf_tensor(f"{name}{i}", [P, 2048], kind)) for i in range(2)]
                  for name, kind in (("shared_hi", F32R), ("shared_lo", F32R), ("shared_raw", F32))]
        ident, shiftm, maskadd = sb("ident", [P, P]), sb("shiftm", [P, P]), sb("maskadd", [P, P])
        rows, cols = np.arange(P)[:, None], np.arange(P)[None]
        consts = np.stack([np.eye(P), np.eye(P, k=1), np.where(cols <= rows, 0.0, MASKED)], 1).astype(np.float32)
        consts_dram = nc.inline_tensor(consts, "square_consts").ap()
        rotary_dram = nc.inline_tensor(rotary_factors(), "rotary_factors").ap()
        consts_loaded = ctx.enter_context(nc.semaphore("consts_loaded"))
        with nc.Block() as block:
            @block.sync
            def _(sp):
                for k, tile in enumerate((ident, shiftm, maskadd)):
                    sp.dma_start(tile[:], consts_dram[:, k]).then_inc(consts_loaded, 16)
                sp.wait_ge(consts_loaded, 48)
        tabs = (ident, shiftm, maskadd, rotary_dram)
        nx, na = 2 + len(_X), 2 + len(_X) + len(_A)
        with ExitStack() as part:
            Wqkv = ins[na + _F.index("Wqkv")]
            ahead = [Wqkv[0].rearrange("(t p) n -> p t n", p=P)[:, :, 1024 * part_no + 512 * half:][:, :, 0:512]
                     for _, part_no, half in CHUNKS_AHEAD]
            two_attentions(nc, part, tabs, X, OUTER, shared, ahead, ins[0], ins[1], ins[2:nx], ins[nx:na])
        with ExitStack() as part:
            local_transformer(nc, part, tabs, X, OUTER, shared, out, ins[na:])


def kernel(**inputs):
    import numpy as _np
    import concourse.bacc as _bacc
    from concourse import mybir as _mybir
    from concourse.bass_utils import run_bass_kernel_spmd as _run

    nc = _bacc.Bacc("TRN2", target_bir_lowering=False, num_devices=1)
    arrays, args = {}, []
    for name in _INS:
        a = _np.ascontiguousarray(inputs[name])
        arrays[f"in_{name}_dram"] = a
        args.append(nc.dram_tensor(f"in_{name}_dram", a.shape, _mybir.dt.from_np(a.dtype), kind="ExternalInput").ap())
    out = nc.dram_tensor("out_0_dram", inputs["x"].shape, _mybir.dt.from_np(_np.dtype("float32")),
                         kind="ExternalOutput").ap()
    perceiver_block(nc, args, out)
    r = _run(nc, [arrays], core_ids=[0])
    return r.results[0]["out_0_dram"]
```
